# Optimizing a Trainium2 kernel written in Bass

```python
import numpy as np
import jax
import jax.numpy as jnp

def _softmax(x, axis=-1):
    return jax.nn.softmax(x, axis=axis)

def _gelu(x):
    return jax.nn.gelu(x, approximate=True)

def _silu(x):
    return jax.nn.silu(x)

def _sigmoid(x):
    return jax.nn.sigmoid(x)

def _layernorm(x, axis=-1, eps=1e-05):
    m = jnp.mean(x, axis=axis, keepdims=True)
    v = jnp.var(x, axis=axis, keepdims=True)
    return (x - m) / jnp.sqrt(v + eps)

def _scatter_add(tgt, idx, src, axis=0):
    return tgt.at[idx].add(src)

def _segment_sum(src, seg, n):
    return jax.ops.segment_sum(src, seg, n)
kernel_name = 'mk_prb_d1_jaxref_r8_66dc09'

def setup_inputs(seed: int=0):
    np.random.seed(seed)
    _w = jnp.asarray

    def _L0_attn_setup():
        import jax, jax.numpy as jnp
        import numpy as np
        LN_EPS = 1e-05

        def _rmsnorm(x, w):
            eps = jnp.finfo(x.dtype).eps
            return x * jax.lax.rsqrt(jnp.mean(x * x, axis=-1, keepdims=True) + eps) * w

        def _layernorm(x, w, b):
            mu = jnp.mean(x, axis=-1, keepdims=True)
            var = jnp.mean((x - mu) ** 2, axis=-1, keepdims=True)
            return (x - mu) * jax.lax.rsqrt(var + LN_EPS) * w + b

        def _gated_delta_rule_scan(q, k, v, lam_h, beta_h):
            B, L, H, d = q.shape
            qT = jnp.moveaxis(q, 1, 0)
            kT = jnp.moveaxis(k, 1, 0)
            vT = jnp.moveaxis(v, 1, 0)
            lam = lam_h[None, :, None, None]
            beta = beta_h[None, :, None, None]

            def step(S, inp):
                q_t, k_t, v_t = inp
                S = S * lam
                err = v_t - jnp.einsum('bhk,bhkv->bhv', k_t, S)
                S = S + beta * (k_t[..., :, None] * err[..., None, :])
                o_t = jnp.einsum('bhk,bhkv->bhv', q_t, S)
                return (S, o_t)
            S0 = jnp.zeros((B, H, d, d), dtype=q.dtype)
            _, o = jax.lax.scan(step, S0, (qT, kT, vT))
            return jnp.moveaxis(o, 0, 1)

        def _apan_forward(x, W, k_norm_w, o_norm_w, o_norm_b, eta_raw, lam_logit):
            B, L, D = x.shape
            H = eta_raw.shape[0]
            d = D // H
            lam = jax.nn.sigmoid(lam_logit)
            eta = jnp.tanh(eta_raw)
            x_act = x
            static_out = x_act @ W.T
            k = _rmsnorm(x_act.reshape(B, L, H, d), k_norm_w)
            q = k
            v_neg = -static_out.reshape(B, L, H, d)
            beta_neg = -(eta * (1.0 - lam) / d)
            o_dyn = _gated_delta_rule_scan(q, k, v_neg, lam, beta_neg)
            return _layernorm(static_out + o_dyn.reshape(B, L, D), o_norm_w, o_norm_b)
        key = jax.random.key(seed)
        k0, k1 = jax.random.split(key)
        B, L, D, H = (4, 256, 128, 16)
        x = jax.random.normal(k0, (B, L, D), dtype=jnp.float32)
        W = jax.random.normal(k1, (D, D), dtype=jnp.float32) / np.sqrt(D)
        k_norm_w = jnp.ones((D // H,), dtype=jnp.float32)
        o_norm_w = jnp.ones((D,), dtype=jnp.float32)
        o_norm_b = jnp.zeros((D,), dtype=jnp.float32)
        eta_raw = jnp.full((H,), float(np.arctanh(0.5)), dtype=jnp.float32)
        lam_logit = jnp.full((H,), float(np.log(0.99 / 0.01)), dtype=jnp.float32)
        return {'x': x, 'W': W, 'k_norm_w': k_norm_w, 'o_norm_w': o_norm_w, 'o_norm_b': o_norm_b, 'eta_raw': eta_raw, 'lam_logit': lam_logit}
    _L0_attn_in = _L0_attn_setup()

    def _L0_ffn_setup():
        import jax, jax.numpy as jnp
        import numpy as np
        TOP_K = 2

        def _mlp(x, w_fc, w_proj):
            return jnp.square(jax.nn.relu(x @ w_fc.T)) @ w_proj.T
        key = jax.random.key(seed)
        ks = jax.random.split(key, 6)
        B, S, D, E = (4, 256, 128, 8)
        d_ff = 4 * D
        x = jax.random.normal(ks[0], (B, S, D), dtype=jnp.float32)
        router_w = jax.random.normal(ks[1], (E, D), dtype=jnp.float32) * 0.02
        w_fc = jax.random.normal(ks[2], (E, d_ff, D), dtype=jnp.float32) * 0.02
        w_proj = jax.random.normal(ks[3], (E, D, d_ff), dtype=jnp.float32) * 0.02
        shared_fc = jax.random.normal(ks[4], (d_ff, D), dtype=jnp.float32) * 0.02
        shared_proj = jax.random.normal(ks[5], (D, d_ff), dtype=jnp.float32) * 0.02
        return {'x': x, 'router_w': router_w, 'w_fc': w_fc, 'w_proj': w_proj, 'shared_fc': shared_fc, 'shared_proj': shared_proj}
    _L0_ffn_in = _L0_ffn_setup()
    _d = {'L0_attn_x': _L0_attn_in['x'], 'L0_attn_W': _L0_attn_in['W'], 'L0_attn_k_norm_w': _L0_attn_in['k_norm_w'], 'L0_attn_o_norm_w': _L0_attn_in['o_norm_w'], 'L0_attn_o_norm_b': _L0_attn_in['o_norm_b'], 'L0_attn_eta_raw': _L0_attn_in['eta_raw'], 'L0_attn_lam_logit': _L0_attn_in['lam_logit'], 'L0_ffn_router_w': _L0_ffn_in['router_w'], 'L0_ffn_w_fc': _L0_ffn_in['w_fc'], 'L0_ffn_w_proj': _L0_ffn_in['w_proj'], 'L0_ffn_shared_fc': _L0_ffn_in['shared_fc'], 'L0_ffn_shared_proj': _L0_ffn_in['shared_proj']}
    _x0 = _d['L0_attn_x']
    _d['L0_attn_x'] = jax.random.normal(jax.random.fold_in(jax.random.key(seed), 1), (4, 1024, 128), dtype=_x0.dtype)
    del _x0
    return _d

def reference(L0_attn_x, L0_attn_W, L0_attn_k_norm_w, L0_attn_o_norm_w, L0_attn_o_norm_b, L0_attn_eta_raw, L0_attn_lam_logit, L0_ffn_router_w, L0_ffn_w_fc, L0_ffn_w_proj, L0_ffn_shared_fc, L0_ffn_shared_proj):

    def _L0_attn_ref(x, W, k_norm_w, o_norm_w, o_norm_b, eta_raw, lam_logit):
        import jax, jax.numpy as jnp
        import numpy as np
        LN_EPS = 1e-05

        def _rmsnorm(x, w):
            eps = jnp.finfo(x.dtype).eps
            return x * jax.lax.rsqrt(jnp.mean(x * x, axis=-1, keepdims=True) + eps) * w

        def _layernorm(x, w, b):
            mu = jnp.mean(x, axis=-1, keepdims=True)
            var = jnp.mean((x - mu) ** 2, axis=-1, keepdims=True)
            return (x - mu) * jax.lax.rsqrt(var + LN_EPS) * w + b

        def _gated_delta_rule_scan(q, k, v, lam_h, beta_h):
            B, L, H, d = q.shape
            qT = jnp.moveaxis(q, 1, 0)
            kT = jnp.moveaxis(k, 1, 0)
            vT = jnp.moveaxis(v, 1, 0)
            lam = lam_h[None, :, None, None]
            beta = beta_h[None, :, None, None]

            def step(S, inp):
                q_t, k_t, v_t = inp
                S = S * lam
                err = v_t - jnp.einsum('bhk,bhkv->bhv', k_t, S)
                S = S + beta * (k_t[..., :, None] * err[..., None, :])
                o_t = jnp.einsum('bhk,bhkv->bhv', q_t, S)
                return (S, o_t)
            S0 = jnp.zeros((B, H, d, d), dtype=q.dtype)
            _, o = jax.lax.scan(step, S0, (qT, kT, vT))
            return jnp.moveaxis(o, 0, 1)

        def _apan_forward(x, W, k_norm_w, o_norm_w, o_norm_b, eta_raw, lam_logit):
            B, L, D = x.shape
            H = eta_raw.shape[0]
            d = D // H
            lam = jax.nn.sigmoid(lam_logit)
            eta = jnp.tanh(eta_raw)
            x_act = x
            static_out = x_act @ W.T
            k = _rmsnorm(x_act.reshape(B, L, H, d), k_norm_w)
            q = k
            v_neg = -static_out.reshape(B, L, H, d)
            beta_neg = -(eta * (1.0 - lam) / d)
            o_dyn = _gated_delta_rule_scan(q, k, v_neg, lam, beta_neg)
            return _layernorm(static_out + o_dyn.reshape(B, L, D), o_norm_w, o_norm_b)
        return _apan_forward(x, W, k_norm_w, o_norm_w, o_norm_b, eta_raw, lam_logit)

    def _L0_ffn_ref(x, router_w, w_fc, w_proj, shared_fc, shared_proj):
        import jax, jax.numpy as jnp
        import numpy as np
        TOP_K = 2

        def _mlp(x, w_fc, w_proj):
            return jnp.square(jax.nn.relu(x @ w_fc.T)) @ w_proj.T
        B, S, D = x.shape
        E = router_w.shape[0]
        T = B * S
        flat = x.reshape(T, D)
        logits = flat @ router_w.T
        probs = jax.nn.softmax(logits.astype(jnp.float32), axis=-1)
        topk_p, topk_i = jax.lax.top_k(probs, TOP_K)
        topk_w = (topk_p / jnp.maximum(topk_p.sum(-1, keepdims=True), 1e-09)).astype(flat.dtype)
        combine = jnp.zeros((T, E), dtype=flat.dtype)
        combine = combine.at[jnp.arange(T)[:, None], topk_i].add(topk_w)
        out = jnp.zeros_like(flat)
        for e in range(E):
            out = out + _mlp(flat, w_fc[e], w_proj[e]) * combine[:, e:e + 1]
        out = out + _mlp(flat, shared_fc, shared_proj)
        return out.reshape(B, S, D)
    x = L0_attn_x
    xn = _layernorm(x, axis=-1)
    x = x + _L0_attn_ref(xn, L0_attn_W, L0_attn_k_norm_w, L0_attn_o_norm_w, L0_attn_o_norm_b, L0_attn_eta_raw, L0_attn_lam_logit) + _L0_ffn_ref(xn, L0_ffn_router_w, L0_ffn_w_fc, L0_ffn_w_proj, L0_ffn_shared_fc, L0_ffn_shared_proj)
    return x

_drawn_inputs = setup_inputs


def setup_inputs(seed=0):
    import zlib

    import numpy as np

    out = dict(_drawn_inputs(seed))
    spreads = {'L0_attn_k_norm_w': (1.0, 0.6),
     'L0_attn_o_norm_w': (1.0, 0.2),
     'L0_attn_o_norm_b': (0.0, 0.1),
     'L0_attn_eta_raw': (0.5493061542510986, 0.6),
     'L0_attn_lam_logit': (4.595119953155518, 0.6)}
    factors = {'L0_ffn_router_w': 4.625,
     'L0_ffn_w_fc': 4.43,
     'L0_ffn_w_proj': 4.065,
     'L0_ffn_shared_fc': 3.125,
     'L0_ffn_shared_proj': 2.856}
    for name, (base, spread) in spreads.items():
        noise = np.random.default_rng([zlib.crc32(name.encode()), seed]).standard_normal(out[name].shape)
        drawn = base * np.exp(spread * noise) if base else spread * noise
        out[name] = jnp.asarray(drawn.astype(out[name].dtype))
    for name, factor in factors.items():
        out[name] = (out[name] * factor).astype(out[name].dtype)
    return out
```

```python
import numpy as np

import concourse.bass as bass
import concourse.mybir as mybir

F32 = mybir.dt.float32
ALU = mybir.AluOpType
ACT = mybir.ActivationFunctionType
AX = mybir.AxisListType

P = 128
B, L, D, H = 4, 1024, 128, 16
HD = D // H
E, FF = 8, 512
SH = E
FC = FF // P
TB = 16
TS = 2 * TB
NT = L // TS
NB = L // TB
LN_EPS = 1e-5
RMS_EPS = float(np.finfo(np.float32).eps)


class Count:

    def __init__(self, sem):
        self.sem, self.n = sem, 0

    def up(self, ins):
        ins.then_inc(self.sem, 1)
        self.n += 1
        return self.n


def build(nc, x, wT, knw, onw, onb, eta, lam, rwT, fcT, pjT, out):
    from contextlib import ExitStack
    with ExitStack() as ctx:
        def sb(name, shape, dt=F32):
            return ctx.enter_context(nc.sbuf_tensor(name, shape, dt))

        def sem(name):
            return ctx.enter_context(nc.semaphore(name))

        xs = sb("xs", [P, NT, D])
        xn = sb("xn", [P, NT, D])
        kn = sb("kn", [P, NT, D])
        tmp = sb("tmp", [P, NT * D])
        xnT = sb("xnT", [P, NT, P])
        KT = sb("KT", [P, TB, B * NB])
        GY = sb("GY", [P, TB, 2, B * NB])
        U = [tmp[:, NT * D // 2 + 2 * D * i:NT * D // 2 + 2 * D * (i + 1)].rearrange("p (r d) -> p r d", r=2) for i in range(2)]
        w_sb = sb("w_sb", [P, D])
        rw_sb = sb("rw_sb", [P, E])
        knw_sb = sb("knw_sb", [P, HD])
        onw_sb = sb("onw_sb", [P, D])
        onb_sb = sb("onb_sb", [P, D])
        eta_sb = sb("eta_sb", [P, 1])
        lam_sb = sb("lam_sb", [P, 1])
        fc_sb = [sb(f"fc{e}", [P, FF]) for e in range(E + 1)]
        pj_sb = [sb(f"pj{e}", [P, FC, D]) for e in range(E + 1)]
        ident = sb("ident", [P, P])
        same = sb("same", [P, P])
        headsum = sb("headsum", [P, TB, P])
        decay = sb("decay", [P, P])
        powr = sb("powr", [P, TB + 1])
        cpow = sb("cpow", [P, TB + 1])
        small = sb("small", [P, 8])
        keyw = sb("keyw", [P, 2 * B + 1, D])
        keywT = sb("keywT", [P, 2, P])
        half = sb("half", [P, 2])
        st = sb("st", [P, 4, NT])
        ks = sb("ks", [P, 2, NT * H])
        fac = sb("fac", [P, NT, H])
        pr = sb("pr", [P, NT, E])
        pa = sb("pa", [P, NT, E])
        pb = sb("pb", [P, NT, E])
        rank = sb("rank", [P, E])
        comb = sb("comb", [P, NT, E])
        KP = [sb(f"KP{i}", [P, TB - 1, NB]) for i in range(2)]
        R = sb("R", [P, B, D])
        YS = [sb(f"YS{i}", [P, P]) for i in range(2)]
        GS = [sb(f"GS{i}", [P, P]) for i in range(2)]
        KM = [xn[:, 8 * i:8 * i + 8, :] for i in range(2)]
        G0 = [sb(f"G0{i}", [P, D]) for i in range(2)]
        hr = [xn[:, 16 + 4 * i:20 + 4 * i, :].rearrange("p i d -> p (i d)") for i in range(2)]
        hs = [xn[:, 24 + 4 * i:28 + 4 * i, :].rearrange("p i d -> p (i d)") for i in range(2)]
        yb = sb("yb", [P, D])
        yst = sb("yst", [P, 6])
        ymv = sb("ymv", [P, 4])
        ysd = sb("ysd", [P, 1])
        acc = sb("acc", [P, 2, D])
        yo = [sb(f"yo{i}", [P, D]) for i in range(2)]

        ps = [ctx.enter_context(nc.psum_tensor(f"ps{i}", [P, 1024], F32)) for i in range(4)]
        pst = [ps[0][:, 0:512], ps[0][:, 512:1024], ps[1][:, 0:512], ps[1][:, 512:1024]]
        pslog = ps[2][:, 0:NT * E]
        pskw = ps[3][:, 0:2 * P]
        psH = [ps[0][:, 0:512], ps[0][:, 512:1024]]
        psY = [ps[1][:, 0:D], ps[1][:, 512:512 + D]]
        psG = ps[2][:, 512:512 + D]
        psU = ps[2][:, 0:D]
        psR = ps[3][:, 0:512]

        x_in, w_in, const_in, head_in = sem("x_in"), sem("w_in"), sem("const_in"), sem("head_in")
        fc_in, pj_in = sem("fc_in"), sem("pj_in")
        masks_made = sem("masks_made")
        lam_act, const_made, keywT_made, keyw_moved = sem("lam_act"), sem("const_made"), sem("keywT_made"), sem("keyw_moved")
        cent_made, sq_made, var_made, sd_made = sem("cent_made"), sem("sq_made"), sem("var_made"), sem("sd_made")
        xn_made, kn_made, kn_sq = sem("xn_made"), sem("kn_made"), sem("kn_sq")
        xnT_ps, xnT_made = sem("xnT_ps"), sem("xnT_made")
        kT_ps, kT_made = sem("kT_ps"), sem("kT_made")
        stat_ps, stat_made, y0_made = sem("stat_ps"), sem("stat_made"), sem("y0_made")
        logits_ps, max_made, exp_made, comb_made = sem("logits_ps"), sem("max_made"), sem("exp_made"), sem("comb_made")
        kp_made, gram_ps, gram_used, gy_made = sem("kp_made"), sem("gram_ps"), sem("gram_used"), sem("gy_made")
        staged, g0_ps, g0_made = sem("staged"), sem("g0_ps"), sem("g0_made")
        u_ps, u_made, r_ps, r_made = sem("u_ps"), sem("u_made"), sem("r_ps"), sem("r_made")
        h_ps, h_relu, h_made, y_ps, y_used = sem("h_ps"), sem("h_relu"), sem("h_made"), sem("y_ps"), sem("y_used")
        yvar_made, ysd_made, yo_made = sem("yvar_made"), sem("ysd_made"), sem("yo_made")
        out_done = [sem(f"out_done{i}") for i in range(2)]
        dve_c, act_c, pool_c = sem("dve_c"), sem("act_c"), sem("pool_c")

        def tile_cols(t3):
            return t3.rearrange("p t (b i r) -> p b i r t", b=B, r=2)

        KTv = tile_cols(KT[:, :, :])
        Gv = tile_cols(GY[:, :, 0, :])
        Yv = tile_cols(GY[:, :, 1, :])

        def head_col(ap):
            return ap.rearrange("(h o) -> h o", o=1).to_broadcast([H, HD])

        block = ctx.enter_context(nc.Block())

        @block.sync
        def _(sp):
            sp.dma_start(lam_sb[:, :], head_col(lam)).then_inc(head_in, 16)
            sp.dma_start(eta_sb[:, :], head_col(eta)).then_inc(head_in, 16)
            for b in range(B):
                sp.dma_start(xs[b * TS:(b + 1) * TS, :, :],
                             x[b].rearrange("(i q) d -> q i d", q=TS)).then_inc(x_in, 16)
            sp.dma_start(knw_sb[:, :], knw.rearrange("(o k) -> o k", o=1).to_broadcast([P, HD])).then_inc(const_in, 16)
            sp.dma_start(onw_sb[:, :], onw.rearrange("(o k) -> o k", o=1).to_broadcast([P, D])).then_inc(const_in, 16)
            sp.dma_start(onb_sb[:, :], onb.rearrange("(o k) -> o k", o=1).to_broadcast([P, D])).then_inc(const_in, 16)
            sp.dma_start(w_sb[:, :], wT).then_inc(w_in, 16)
            sp.dma_start(rw_sb[:, :], rwT).then_inc(w_in, 16)
            for e in [SH] + list(range(E)):
                sp.dma_start(fc_sb[e][:, :], fcT[:, e, :]).then_inc(fc_in, 16)
                sp.dma_start(pj_sb[e][:, :, :], pjT[:, e, :, :]).then_inc(pj_in, 16)
            with sp.Fori(0, NT // 2) as it:
                for u in range(2):
                    sp.wait_ge(yo_made, it * 2 + (u + 1))
                    for b in range(B):
                        sp.dma_start(out[b].rearrange("(i q) d -> i q d", q=TS)[bass.ds(it * 2 + u, 1)].rearrange("o q d -> (o q) d"),
                                     yo[u][b * TS:(b + 1) * TS, :]).then_inc(out_done[u], 16)
            for u in range(2):
                sp.wait_ge(out_done[u], NT // 2 * B * 16)

        @block.gpsimd
        def _(pool):
            m = Count(masks_made)
            m.up(nc.gpsimd.memset(ident[:, :], 0.0))
            m.up(nc.gpsimd.memset(same[:, :], 1.0))
            m.up(nc.gpsimd.iota(rank[:, :], pattern=[[-1, E]], base=E, channel_multiplier=0,
                                allow_small_or_imprecise_dtypes=True))
            pool.wait_ge(masks_made, m.n)
            m.up(nc.gpsimd.affine_select(out=ident[:, :], in_=ident[:, :], compare_op=ALU.not_equal, fill=1.0,
                                         base=0, pattern=[[-1, P]], channel_multiplier=1))
            sv = same[:, :].rearrange("p (h k) -> p h k", k=HD)
            m.up(nc.gpsimd.affine_select(out=sv, in_=sv, compare_op=ALU.is_ge, fill=0.0,
                                         base=0, pattern=[[-HD, H], [0, HD]], channel_multiplier=1))
            pool.wait_ge(masks_made, m.n)
            m.up(nc.gpsimd.affine_select(out=sv, in_=sv, compare_op=ALU.is_ge, fill=0.0,
                                         base=HD - 1, pattern=[[HD, H], [0, HD]], channel_multiplier=-1))
            m.up(nc.gpsimd.memset(R[:, :, :], 0.0))
            m.up(nc.gpsimd.memset(keyw[:, 0:2 * B, :], 0.0))
            assert m.n == MASKS

            pool.wait_ge(kT_made, NT)
            with pool.Fori(0, B) as b:
                cols = bass.ds(b * NB, NB)
                for s in range(TB - 1):
                    n = TB - 1 - s
                    if s >= 2:
                        pool.wait_ge(gram_ps, b * (TB - 1) + (s - 1))
                    else:
                        pool.wait_ge(gram_used, b * (TB - 1))
                    nc.gpsimd.tensor_tensor(KP[s % 2][:, 0:n, :], KT[:, s + 1:TB, cols],
                                            KT[:, s:s + 1, cols].to_broadcast([P, n, NB]), ALU.mult).then_inc(kp_made, 1)

            pool.wait_ge(gy_made, B * (TB - 1))
            pool.wait_ge(keyw_moved, 3)
            with pool.Fori(0, NT // 2) as it:
                for u in range(2):
                    i = it * 2 + u
                    if u == 0:
                        pool.wait_ge(r_made, it * 4)
                    else:
                        pool.wait_ge(r_made, it * 4)
                    for dst, src in ((GS[u], Gv), (YS[u], Yv)):
                        for b in range(B):
                            nc.gpsimd.tensor_copy(dst[:, b * TS:(b + 1) * TS].rearrange("p (r t) -> p r t", r=2),
                                                  src[:, b, bass.ds(i, 1)].rearrange("p o r t -> p (o r) t")).then_inc(staged, 1)
                    nc.gpsimd.tensor_tensor(KM[u], kn[:, bass.ds(i, 1), :].to_broadcast([P, 2 * B, D]),
                                            keyw[:, 0:2 * B, :], ALU.mult).then_inc(staged, 1)

        @block.scalar
        def _(act):
            act.wait_ge(head_in, 32)
            nc.scalar.activation(small[:, 0:1], lam_sb[:, :], ACT.Exp, scale=-1.0).then_inc(lam_act, 1)
            nc.scalar.activation(small[:, 1:2], eta_sb[:, :], ACT.Tanh).then_inc(lam_act, 1)
            act.wait_ge(cent_made, 1)
            nc.scalar.activation(tmp[:, :], xn[:, :, :].rearrange("p i d -> p (i d)"), ACT.Square).then_inc(sq_made, 1)
            act.wait_ge(var_made, 1)
            nc.scalar.activation(st[:, 2, :], st[:, 1, :], ACT.Sqrt).then_inc(sd_made, 1)
            act.wait_ge(xn_made, 1)
            nc.scalar.activation(tmp[:, :], xn[:, :, :].rearrange("p i d -> p (i d)"), ACT.Square).then_inc(sq_made, 1)
            for g in range(NT // 4):
                act.wait_ge(xnT_ps, g + 1)
                nc.scalar.copy(xnT[:, 4 * g:4 * g + 4, :].rearrange("p i t -> p (i t)"), pst[g % 2]).then_inc(xnT_made, 1)
            act.wait_ge(var_made, 2)
            nc.scalar.activation(ks[:, 1, :], ks[:, 0, :], ACT.Sqrt).then_inc(sd_made, 1)
            act.wait_ge(kn_made, 1)
            nc.scalar.activation(tmp[:, :], kn[:, :, :].rearrange("p i d -> p (i d)"), ACT.Square).then_inc(sq_made, 1)
            for i in range(NT):
                if i % 4 == 0:
                    act.wait_ge(kT_ps, i // 4 + 1)
                nc.scalar.copy(KTv[:, :, i], pst[2 + i // 4 % 2][:, P * (i % 4):P * (i % 4 + 1)]
                               .rearrange("p (b r t) -> p b r t", b=B, r=2)).then_inc(kT_made, 1)
            for i in range(NT):
                if i % 4 == 0:
                    act.wait_ge(stat_ps, i // 4 + 1)
                nc.scalar.copy(Gv[:, :, i], pst[i // 4 % 2][:, P * (i % 4):P * (i % 4 + 1)]
                               .rearrange("p (b r t) -> p b r t", b=B, r=2)).then_inc(stat_made, 1)
            act.wait_ge(const_made, CONSTS)
            act.wait_ge(kT_made, NT)
            for t in range(TB):
                nc.scalar.activation(GY[:, t, 1, :], KT[:, t, :], ACT.Copy, scale=powr[:, t + 1:t + 2]).then_inc(y0_made, 1)
            act.wait_ge(max_made, 1)
            nc.scalar.activation(pa[:, :, :], pr[:, :, :], ACT.Exp).then_inc(exp_made, 1)

            with act.Fori(0, NT // 2) as it:
                for u in range(2):
                    for n in range(E + 1):
                        k = u * (E + 1) + n
                        unit = it * (2 * (E + 1)) + k
                        act.wait_ge(h_ps, unit + 1)
                        nc.scalar.activation(hr[k % 2][:, :], psH[k % 2], ACT.Relu).then_inc(h_relu, 1)
                        if k >= 2:
                            act.wait_ge(y_ps, unit - 1)
                        else:
                            act.wait_ge(y_used, it * (2 * (E + 1)))
                        act.wait_ge(h_relu, unit + 1)
                        nc.scalar.activation(hs[k % 2][:, :], hr[k % 2][:, :], ACT.Square).then_inc(h_made, 1)
                        if n == 0:
                            act.wait_ge(g0_ps, it * 2 + (u + 1))
                            nc.scalar.copy(G0[u][:, :], psG).then_inc(g0_made, 1)
                        if n == E:
                            act.wait_ge(yvar_made, it * 2 + (u + 1))
                            nc.scalar.activation(ysd[:, :], ymv[:, 2:3], ACT.Sqrt).then_inc(ysd_made, 1)

        @block.vector
        def _(dve):
            c = Count(dve_c)

            def link(ins):
                dve.wait_ge(dve_c, c.up(ins))

            v = nc.vector
            q = Count(const_made)

            def qlink(ins):
                dve.wait_ge(const_made, q.up(ins))

            dve.wait_ge(masks_made, MASKS)
            dve.wait_ge(lam_act, 2)
            qlink(v.tensor_scalar(small[:, 2:3], small[:, 0:1], 1.0, None, ALU.add))
            q.up(v.memset(powr[:, 0:1], 1.0))
            qlink(v.reciprocal(powr[:, 1:2], small[:, 2:3]))
            qlink(v.tensor_scalar(small[:, 3:4], powr[:, 1:2], -1.0, 1.0, ALU.mult, ALU.add))
            qlink(v.tensor_scalar(small[:, 4:5], small[:, 3:4], small[:, 1:2], 1.0 / HD, ALU.mult, ALU.mult))
            for n in range(2, TB + 1):
                qlink(v.tensor_scalar(powr[:, n:n + 1], powr[:, n - 1:n], powr[:, 1:2], None, ALU.mult))
            qlink(v.tensor_scalar(cpow[:, :], powr[:, :], small[:, 4:5], None, ALU.mult))
            q.up(v.tensor_scalar(decay[:, :], ident[:, :], powr[:, TB:TB + 1], None, ALU.mult))
            q.up(v.tensor_tensor(headsum[:, :, :], same[:, :].unsqueeze(1).to_broadcast([P, TB, P]),
                                 cpow[:, 0:TB].unsqueeze(2).to_broadcast([P, TB, P]), ALU.mult))
            for t in range(TB):
                q.up(v.tensor_copy(keywT[:, 0, :].rearrange("p (a t) -> p a t", t=TB)[:, :, t:t + 1],
                                   cpow[:, TB - 1 - t:TB - t].unsqueeze(1).to_broadcast([P, P // TB, 1])))
            q.up(v.tensor_copy(keywT[:, 1, :], small[:, 4:5].to_broadcast([P, P])))
            assert q.n == CONSTS

            dve.wait_ge(x_in, 64)
            link(v.tensor_reduce(st[:, 0, :], xs[:, :, :], AX.X, ALU.add))
            link(v.tensor_scalar(st[:, 3, :], st[:, 0, :], 1.0 / D, None, ALU.mult))
            v.tensor_tensor(xn[:, :, :], xs[:, :, :], st[:, 3, :].unsqueeze(2).to_broadcast([P, NT, D]),
                            ALU.subtract).then_inc(cent_made, 1)
            dve.wait_ge(sq_made, 1)
            link(v.tensor_reduce(st[:, 0, :], tmp[:, :].rearrange("p (i d) -> p i d", d=D), AX.X, ALU.add))
            v.tensor_scalar(st[:, 1, :], st[:, 0, :], 1.0 / D, LN_EPS, ALU.mult, ALU.add).then_inc(var_made, 1)
            dve.wait_ge(sd_made, 1)
            link(v.reciprocal(st[:, 3, :], st[:, 2, :]))
            dve.wait_ge(cent_made, 1)
            v.tensor_tensor(xn[:, :, :], xn[:, :, :], st[:, 3, :].unsqueeze(2).to_broadcast([P, NT, D]),
                            ALU.mult).then_inc(xn_made, 1)
            dve.wait_ge(sq_made, 2)
            link(v.tensor_reduce(ks[:, 1, :], tmp[:, :].rearrange("p (i k) -> p i k", k=HD), AX.X, ALU.add))
            v.tensor_scalar(ks[:, 0, :], ks[:, 1, :], 1.0 / HD, RMS_EPS, ALU.mult, ALU.add).then_inc(var_made, 1)
            dve.wait_ge(sd_made, 2)
            link(v.reciprocal(ks[:, 0, :], ks[:, 1, :]))
            dve.wait_ge(xn_made, 1)
            knv = kn[:, :, :].rearrange("p i (h k) -> p (i h) k", k=HD)
            link(v.tensor_tensor(knv, xn[:, :, :].rearrange("p i (h k) -> p (i h) k", k=HD),
                                 ks[:, 0, :].unsqueeze(2).to_broadcast([P, NT * H, HD]), ALU.mult))
            dve.wait_ge(const_in, 3 * 16)
            v.tensor_tensor(knv, knv, knw_sb[:, :].unsqueeze(1).to_broadcast([P, NT * H, HD]),
                            ALU.mult).then_inc(kn_made, 1)
            dve.wait_ge(keywT_made, 1)
            k3 = Count(keyw_moved)
            k3.up(v.tensor_copy(keyw[:, 2 * B, :], pskw[:, P:2 * P]))
            k3.up(v.tensor_reduce(half[:, 0:1], ident[:, :].rearrange("p (b r t) -> p b r t", b=B, r=2)[:, :, 0, :],
                                  AX.XY, ALU.add))
            dve.wait_ge(keyw_moved, 2)
            link(v.tensor_scalar(half[:, 1:2], half[:, 0:1], -1.0, 1.0, ALU.mult, ALU.add))
            for b in range(B):
                rows = slice(b * TS, (b + 1) * TS)
                for r in range(2):
                    ins = v.tensor_scalar(keyw[rows, r * B + b, :], pskw[rows, 0:P], half[rows, r:r + 1], None, ALU.mult)
                    if b < B - 1 or r == 0:
                        c.up(ins)
            k3.up(ins)
            dve.wait_ge(sq_made, 3)
            link(v.tensor_reduce(ks[:, 0, :], tmp[:, :].rearrange("p (i k) -> p i k", k=HD), AX.X, ALU.add))
            link(v.tensor_tensor(fac[:, :, :], ks[:, 0, :].rearrange("p (i h) -> p i h", h=H),
                                 keyw[:, 2 * B, :].rearrange("p (h k) -> p k h", k=HD)[:, 0:1, :]
                                 .to_broadcast([P, NT, H]), ALU.mult))
            link(v.tensor_scalar(fac[:, :, :], fac[:, :, :], 1.0, None, ALU.add))

            def over_e(ap):
                return ap.unsqueeze(2).to_broadcast([P, NT, E])

            dve.wait_ge(logits_ps, 1)
            lg = pslog.rearrange("p (i e) -> p i e", e=E)
            link(v.tensor_reduce(st[:, 0, :], lg, AX.X, ALU.max))
            v.tensor_tensor(pr[:, :, :], lg, over_e(st[:, 0, :]), ALU.subtract).then_inc(max_made, 1)
            dve.wait_ge(exp_made, 1)
            link(v.tensor_reduce(st[:, 0, :], pa[:, :, :], AX.X, ALU.add))
            link(v.reciprocal(st[:, 1, :], st[:, 0, :]))
            link(v.tensor_tensor(pr[:, :, :], pa[:, :, :], over_e(st[:, 1, :]), ALU.mult))
            rankb = rank[:, :].unsqueeze(1).to_broadcast([P, NT, E])
            for k in range(2):
                link(v.tensor_reduce(st[:, k, :], pr[:, :, :], AX.X, ALU.max))
                link(v.tensor_tensor(pb[:, :, :], pr[:, :, :], over_e(st[:, k, :]), ALU.is_equal))
                link(v.tensor_tensor(pb[:, :, :], pb[:, :, :], rankb, ALU.mult))
                link(v.tensor_reduce(st[:, 2, :], pb[:, :, :], AX.X, ALU.max))
                link(v.tensor_tensor(pa[:, :, :], pb[:, :, :], over_e(st[:, 2, :]), ALU.is_equal))
                dst = comb if k == 0 else pb
                link(v.tensor_tensor(dst[:, :, :], pa[:, :, :], over_e(st[:, k, :]), ALU.mult))
                if k == 0:
                    link(v.tensor_tensor(pr[:, :, :], pr[:, :, :], comb[:, :, :], ALU.subtract))
                    link(v.tensor_tensor(pr[:, :, :], pr[:, :, :], pa[:, :, :], ALU.subtract))
            link(v.tensor_tensor(comb[:, :, :], comb[:, :, :], pb[:, :, :], ALU.add))
            link(v.tensor_tensor(st[:, 2, :], st[:, 0, :], st[:, 1, :], ALU.add))
            link(v.tensor_scalar(st[:, 2, :], st[:, 2, :], 1e-9, None, ALU.max))
            link(v.reciprocal(st[:, 3, :], st[:, 2, :]))
            link(v.tensor_tensor(comb[:, :, :], comb[:, :, :], over_e(st[:, 3, :]), ALU.mult))

            dve.wait_ge(stat_made, NT)
            dve.wait_ge(y0_made, TB)
            prod = tmp[:, 0:(TB - 1) * 2 * NB].rearrange("p (t g c) -> p t g c", g=2, c=NB)
            with dve.Fori(0, B) as b:
                cols = bass.ds(b * NB, NB)
                for s in range(TB - 1):
                    n = TB - 1 - s
                    step = b * (TB - 1) + s
                    dve.wait_ge(gram_ps, step + 1)
                    dve.wait_ge(gy_made, step)
                    gram = ps[s % 2][:, 0:n * NB].rearrange("p (t o c) -> p t o c", o=1, c=NB)
                    v.tensor_tensor(prod[:, 0:n], gram.to_broadcast([P, n, 2, NB]),
                                    GY[:, s:s + 1, :, cols].to_broadcast([P, n, 2, NB]), ALU.mult).then_inc(gram_used, 1)
                    dve.wait_ge(gram_used, step + 1)
                    v.tensor_tensor(GY[:, s + 1:TB, :, cols], GY[:, s + 1:TB, :, cols], prod[:, 0:n],
                                    ALU.add).then_inc(gy_made, 1)

            base = c.n
            with dve.Fori(0, NT // 2) as it:
                c.n = 0

                def llink(ins):
                    dve.wait_ge(dve_c, it * LINKS + (base + c.up(ins)))

                for u in range(2):
                    i = it * 2 + u

                    def collect(lo, hi):
                        for n in range(lo, hi):
                            k = u * (E + 1) + n
                            unit = it * (2 * (E + 1)) + k
                            dve.wait_ge(y_ps, unit + 1)
                            if n == 0:
                                dve.wait_ge(yo_made, i)
                                v.tensor_tensor(acc[:, 0, :], psY[k % 2], xs[:, bass.ds(i, 1), :].rearrange("p o d -> p (o d)"),
                                                ALU.add).then_inc(y_used, 1)
                            else:
                                dve.wait_ge(y_used, unit)
                                v.scalar_tensor_tensor(acc[:, n % 2, :], psY[k % 2],
                                                       comb[:, bass.ds(i, 1), n - 1:n].rearrange("p o e -> p (o e)"),
                                                       acc[:, 1 - n % 2, :], ALU.mult, ALU.add).then_inc(y_used, 1)

                    for r in range(2):
                        blk = it * 4 + (u * 2 + r)
                        dve.wait_ge(u_ps, blk + 1)
                        if r == 0:
                            dve.wait_ge(g0_made, it * 2 + (u + 1))
                        v.tensor_tensor(U[u][:, r, :], psU, G0[u][:, :],
                                        ALU.add).then_inc(u_made, 1)
                        collect((0, 4)[r], (2, 6)[r])
                        dve.wait_ge(r_ps, blk + 1)
                        v.tensor_tensor(R[:, :, :], psR.rearrange("p (b d) -> p b d", b=B),
                                        same[:, :].unsqueeze(1).to_broadcast([P, B, D]), ALU.mult).then_inc(r_made, 1)
                        collect((2, 6)[r], (4, 7)[r])
                    dve.wait_ge(u_made, it * 4 + (u * 2 + 2))
                    llink(v.tensor_scalar(yb[:, :], U[u][:, 0, :], half[:, 0:1], None, ALU.mult))
                    llink(v.scalar_tensor_tensor(yb[:, :], U[u][:, 1, :], half[:, 1:2], yb[:, :],
                                                 ALU.mult, ALU.add))
                    ybv = yb[:, :].rearrange("p (h k) -> p h k", k=HD)
                    llink(v.tensor_tensor(ybv, ybv, fac[:, bass.ds(i, 1), :].rearrange("p o h -> p (o h)").unsqueeze(2)
                                          .to_broadcast([P, H, HD]), ALU.mult))
                    llink(v.bn_stats(yst[:, :], yb[:, :]))
                    collect(7, 8)
                    llink(v.bn_aggr(ymv[:, 0:2], yst[:, :]))
                    v.tensor_scalar(ymv[:, 2:3], ymv[:, 1:2], LN_EPS, None, ALU.add).then_inc(yvar_made, 1)
                    collect(8, 9)
                    dve.wait_ge(ysd_made, it * 2 + (u + 1))
                    llink(v.reciprocal(ymv[:, 3:4], ysd[:, :]))
                    llink(v.tensor_scalar(yb[:, :], yb[:, :], ymv[:, 0:1], ymv[:, 3:4], ALU.subtract, ALU.mult))
                    llink(v.tensor_tensor(yb[:, :], yb[:, :], onw_sb[:, :], ALU.mult))
                    llink(v.tensor_tensor(yb[:, :], yb[:, :], onb_sb[:, :], ALU.add))
                    dve.wait_ge(y_used, it * (2 * (E + 1)) + (u + 1) * (E + 1))
                    dve.wait_ge(out_done[u], it * (B * 16))
                    v.tensor_tensor(yo[u][:, :], yb[:, :], acc[:, E % 2, :], ALU.add).then_inc(yo_made, 1)
                assert c.n == LINKS, c.n

        @block.tensor
        def _(pe):
            mm, tr = nc.tensor.matmul, nc.tensor.transpose
            pe.wait_ge(masks_made, MASKS)
            pe.wait_ge(xn_made, 1)
            for g in range(NT // 4):
                if g >= 2:
                    pe.wait_ge(xnT_made, g - 1)
                for j in range(4):
                    ins = tr(pst[g % 2][:, P * j:P * j + P], xn[:, 4 * g + j, :], ident[:, :])
                ins.then_inc(xnT_ps, 1)
            pe.wait_ge(w_in, 32)
            pe.wait_ge(xnT_made, NT // 4)
            for i in range(NT):
                ins = mm(pslog[:, E * i:E * i + E], xnT[:, i, :], rw_sb[:, :], start=True, stop=True)
            ins.then_inc(logits_ps, 1)
            pe.wait_ge(const_made, CONSTS)
            tr(pskw[:, 0:P], keywT[:, 0, :], ident[:, :])
            tr(pskw[:, P:2 * P], keywT[:, 1, :], ident[:, :]).then_inc(keywT_made, 1)
            pe.wait_ge(kn_made, 1)
            for g in range(NT // 4):
                if g >= 2:
                    pe.wait_ge(kT_made, 4 * (g - 1))
                for j in range(4):
                    ins = tr(pst[2 + g % 2][:, P * j:P * j + P], kn[:, 4 * g + j, :], ident[:, :])
                ins.then_inc(kT_ps, 1)
            for g in range(NT // 4):
                if g >= 2:
                    pe.wait_ge(stat_made, 4 * (g - 1))
                mm(pst[g % 2], w_sb[:, :], xnT[:, 4 * g:4 * g + 4, :].rearrange("p i t -> p (i t)"),
                   start=True, stop=True).then_inc(stat_ps, 1)
            pe.wait_ge(stat_made, NT)
            with pe.Fori(0, B) as b:
                for s in range(TB - 1):
                    n = TB - 1 - s
                    step = b * (TB - 1) + s
                    pe.wait_ge(kp_made, step + 1)
                    if s >= 2:
                        pe.wait_ge(gram_used, step - 1)
                    else:
                        pe.wait_ge(gram_used, b * (TB - 1))
                    for t in range(n):
                        ins = mm(ps[s % 2][:, t * NB:(t + 1) * NB], headsum[:, t + 1, :], KP[s % 2][:, t, :],
                                 start=True, stop=True)
                    ins.then_inc(gram_ps, 1)
            pe.wait_ge(gram_used, B * (TB - 1))
            pe.wait_ge(fc_in, 16 * (E + 1))
            pe.wait_ge(pj_in, 16 * (E + 1))

            UNITS = 2 * (E + 1)
            with pe.Fori(0, NT // 2) as it:
                for u in range(2):
                    i = it * 2 + u

                    def up(n):
                        k = u * (E + 1) + n
                        e = SH if n == 0 else n - 1
                        if k >= 2:
                            pe.wait_ge(h_relu, it * UNITS + (k - 1))
                        else:
                            pe.wait_ge(h_relu, it * UNITS)
                        for f in range(FC):
                            ins = mm(psH[k % 2][:, f * P:f * P + P], fc_sb[e][:, f * P:f * P + P],
                                     xnT[:, bass.ds(i, 1), :].rearrange("p o t -> p (o t)"), start=True, stop=True)
                        ins.then_inc(h_ps, 1)

                    def down(n):
                        k = u * (E + 1) + n
                        e = SH if n == 0 else n - 1
                        pe.wait_ge(h_made, it * UNITS + (k + 1))
                        if k >= 2:
                            pe.wait_ge(y_used, it * UNITS + (k - 1))
                        else:
                            pe.wait_ge(y_used, it * UNITS)
                        for f in range(FC):
                            ins = mm(psY[k % 2], hs[k % 2][:, f * P:f * P + P], pj_sb[e][:, f, :],
                                     start=(f == 0), stop=(f == FC - 1))
                        ins.then_inc(y_ps, 1)

                    def units(lo, hi):
                        for n in range(lo, hi):
                            down(n)
                            if n + 2 <= E:
                                up(n + 2)

                    pe.wait_ge(staged, it * 18 + (9 * u + 9))
                    if u == 0:
                        pe.wait_ge(g0_made, it * 2)
                    else:
                        pe.wait_ge(g0_made, it * 2 + 1)
                    tr(psG, GS[u][:, :], ident[:, :]).then_inc(g0_ps, 1)
                    up(0)
                    up(1)
                    for r in range(2):
                        blk = it * 4 + (u * 2 + r)
                        pe.wait_ge(r_made, blk)
                        for b in range(B):
                            ins = mm(psU[b * TS:(b + 1) * TS, :], YS[u][:, b * TS:(b + 1) * TS], R[:, b, :], start=True, stop=True)
                        ins.then_inc(u_ps, 1)
                        units((0, 4)[r], (2, 6)[r])
                        mm(psR, decay[:, :], R[:, :, :].rearrange("p b d -> p (b d)"), start=True, stop=False)
                        pe.wait_ge(u_made, blk + 1)
                        for b in range(B):
                            ins = mm(psR[:, b * D:(b + 1) * D], KM[u][:, r * B + b, :],
                                     U[u][:, r, :], start=False, stop=(b == B - 1))
                        ins.then_inc(r_ps, 1)
                        units((2, 6)[r], (4, 9)[r])


MASKS = 8
CONSTS = 1 + 1 + 3 + (TB - 1) + 1 + 2 + TB + 1
LINKS = 2 * 9


def kernel(L0_attn_x, L0_attn_W, L0_attn_k_norm_w, L0_attn_o_norm_w, L0_attn_o_norm_b, L0_attn_eta_raw,
           L0_attn_lam_logit, L0_ffn_router_w, L0_ffn_w_fc, L0_ffn_w_proj, L0_ffn_shared_fc, L0_ffn_shared_proj):
    import concourse.bacc as bacc
    from concourse.bass_utils import run_bass_kernel_spmd

    def lay(a, order=None):
        a = np.asarray(a)
        return np.ascontiguousarray(a.transpose(order) if order else a)

    fc = np.concatenate([np.asarray(L0_ffn_w_fc), np.asarray(L0_ffn_shared_fc)[None]])
    pj = np.concatenate([np.asarray(L0_ffn_w_proj), np.asarray(L0_ffn_shared_proj)[None]])
    ins = {
        "x": lay(L0_attn_x),
        "wT": lay(L0_attn_W, (1, 0)),
        "knw": lay(L0_attn_k_norm_w), "onw": lay(L0_attn_o_norm_w), "onb": lay(L0_attn_o_norm_b),
        "eta": lay(L0_attn_eta_raw), "lam": lay(L0_attn_lam_logit),
        "rwT": lay(L0_ffn_router_w, (1, 0)),
        "fcT": lay(fc, (2, 0, 1)),
        "pjT": lay(pj.reshape(E + 1, D, FC, P), (3, 0, 2, 1)),
    }
    nc = bacc.Bacc("TRN2", target_bir_lowering=False, num_devices=1)
    aps = [nc.dram_tensor(n, a.shape, mybir.dt.from_np(a.dtype), kind="ExternalInput").ap() for n, a in ins.items()]
    out = nc.dram_tensor("out", (B, L, D), F32, kind="ExternalOutput").ap()
    build(nc, *aps, out)
    r = run_bass_kernel_spmd(nc, [ins], core_ids=[0])
    return r.results[0]["out"]
```

```python
import numpy as np

import concourse.bass as bass
import concourse.mybir as mybir

F32 = mybir.dt.float32
I32 = mybir.dt.int32
U32 = mybir.dt.uint32
ALU = mybir.AluOpType
ACT = mybir.ActivationFunctionType
AX = mybir.AxisListType

P = 128
B, L, D, H = 4, 1024, 128, 16
HD = D // H
E, FF = 8, 512
TOPK = 2
FC = FF // P
TB = 16
TS = 2 * TB
NT = L // TS
NB = NT * B * 2
QT = 4
QB = NB // QT
SLOTS = TOPK * NT + E
AHEAD = 4
SPQ = SLOTS // (QT - 1)
LN_EPS = 1e-5
RMS_EPS = float(np.finfo(np.float32).eps)

WORK = [sum(TB - 1 - j for j in range(k + 1)) for k in range(TB - 1)]
DUE = [round(SPQ * w / WORK[-1]) for w in WORK]
DUE = [list(range(lo, hi)) for lo, hi in zip([0] + DUE[:-1], DUE)]
assert DUE[-1] and DUE[-1][-1] == SPQ - 1 or sum(map(len, DUE)) == SPQ
assert SPQ * (QT - 1) == SLOTS and SPQ % AHEAD == 0


class Count:

    def __init__(self, sem):
        self.sem, self.n = sem, 0

    def up(self, ins):
        ins.then_inc(self.sem, 1)
        self.n += 1
        return self.n


def build(nc, x, wT, knw, onw, onb, eta, lam, rwT, fcT, pjT, sfcT, spjT, out):
    from contextlib import ExitStack
    with ExitStack() as ctx:
        def sb(name, shape, dt=F32):
            return ctx.enter_context(nc.sbuf_tensor(name, shape, dt))

        def sem(name):
            return ctx.enter_context(nc.semaphore(name))

        slot_x = nc.dram_tensor("slot_x", [(SLOTS + AHEAD) * P, D], F32).ap()
        slot_y = nc.dram_tensor("slot_y", [SLOTS * P, D], F32).ap()

        xs = sb("xs", [P, NT, D])
        xn = sb("xn", [P, NT, D])
        kn = sb("kn", [P, NT, D])
        tmp = sb("tmp", [P, NT * D])
        xnT = sb("xnT", [P, NT, P])
        KT = sb("KT", [P, TB, NB])
        GY = sb("GY", [P, TB, 2, NB])
        w_sb = sb("w_sb", [P, D])
        rw_sb = sb("rw_sb", [P, E])
        knw_sb = sb("knw_sb", [P, HD])
        onw_sb = sb("onw_sb", [P, D])
        onb_sb = sb("onb_sb", [P, D])
        eta_sb = sb("eta_sb", [P, 1])
        lam_sb = sb("lam_sb", [P, 1])
        fc_sb = sb("fc_sb", [P, E, FF])
        pj_sb = sb("pj_sb", [P, E, FC, D])
        sfc_sb = sb("sfc_sb", [P, FF])
        spj_sb = sb("spj_sb", [P, FC, D])
        ident = sb("ident", [P, P])
        same = sb("same", [P, P])
        before = sb("before", [P, P])
        ones = sb("ones", [P, P])
        headsum = sb("headsum", [P, TB, P])
        decay = sb("decay", [P, P])
        powr = sb("powr", [P, TB + 1])
        cpow = sb("cpow", [P, TB + 1])
        small = sb("small", [P, 8])
        keyw = sb("keyw", [P, 3, D])
        keywT = sb("keywT", [P, 2, P])
        half = sb("half", [P, 2])
        st = sb("st", [P, 4, NT])
        ks = sb("ks", [P, 2, NT * H])
        fac = sb("fac", [P, NT, H])
        rank = sb("rank", [P, E])
        steps = sb("steps", [P, NT])
        tiles = sb("tiles", [P, 4, E])
        owner = sb("owner", [P, SLOTS + AHEAD], I32)
        wgt = sb("wgt", [P, TOPK, NT])
        pos = sb("pos", [P, NT, TOPK], U32)
        KP = [sb(f"KP{i}", [P, TB - 1, QB]) for i in range(2)]
        R = sb("R", [P, B, D])
        yst = sb("yst", [P, 6])
        ymv = sb("ymv", [P, 4])
        ysd = sb("ysd", [P, 1])

        at = [0]

        def scratch(*shape):
            n = int(np.prod(shape))
            at[0] += n
            ap = GY[:, :, :, :].rearrange("p t g c -> p (t g c)")[:, at[0] - n:at[0]]
            return ap.rearrange("p (a b) -> p a b", b=shape[1]) if len(shape) == 2 else ap

        pr, pb, both = (scratch(NT, E) for _ in range(3))
        pick = [scratch(NT, E) for _ in range(TOPK)]
        total = scratch(NT, E)
        upto, need = scratch(E, NT), scratch(E, NT)
        slot_no, owner_f = scratch(SLOTS + AHEAD), scratch(SLOTS + AHEAD)
        past = scratch(SLOTS + AHEAD, E)
        pos_f = scratch(NT, TOPK)

        def part(t, n):
            at = [0]

            def take(tiles):
                at[0] += tiles
                assert at[0] <= n
                return t[:, at[0] - tiles:at[0], :]
            return take

        def flat(ap):
            return ap.rearrange("p a b -> p (a b)")

        take = part(xn, NT)
        hr = [flat(take(4)) for _ in range(2)]
        hs = [flat(take(4)) for _ in range(2)]
        wst = [flat(take(4)) for _ in range(2)]
        xT = [flat(take(1)) for _ in range(2)]
        ys = [flat(take(1)) for _ in range(2)]
        xg = [flat(take(1)) for _ in range(AHEAD)]
        take = part(tmp[:, :].rearrange("p (i d) -> p i d", d=D)[:, NT // 2:NT, :], NT // 2)
        GS = [flat(take(1)) for _ in range(2)]
        YS = [take(2) for _ in range(2)]
        KS = [take(2) for _ in range(2)]
        U = [sb(f"U{i}", [P, 2, D]) for i in range(2)]
        gy = [[sb(f"gy{i}{k}", [P, D]) for k in range(TOPK)] for i in range(2)]
        acc = flat(take(1))
        yb = flat(take(1))
        yo = [flat(take(1)) for _ in range(2)]
        ix = [sb(f"ix{i}", [P, TOPK], U32) for i in range(2)]

        ps = [ctx.enter_context(nc.psum_tensor(f"ps{i}", [P, 1024], F32)) for i in range(4)]

        def bank(n):
            return ps[n // 2][:, 512 * (n % 2):512 * (n % 2) + 512]

        pst = [bank(0), bank(1), bank(2), bank(3)]
        pslog = bank(4)[:, 0:NT * E]
        pskw = bank(5)[:, 0:2 * P]
        psbefore, pstotal = bank(6)[:, 0:NT * E], bank(7)[:, 0:NT * E]
        psX, psH, psY = bank(4)[:, 0:P], [bank(5), bank(6)], bank(7)[:, 0:D]
        psR = [bank(b)[:, 0:D] for b in range(B)]
        psRv = [ps[n][:, :].rearrange("p (b c) -> p b c", b=2)[:, :, 0:D] for n in range(2)]
        psU = bank(4)[:, 0:D]

        x_in, w_in, const_in, head_in = sem("x_in"), sem("w_in"), sem("const_in"), sem("head_in")
        routed_in, shared_in = sem("routed_in"), sem("shared_in")
        masks_made, iotas_made, zeros_made, cleared = sem("masks_made"), sem("iotas_made"), sem("zeros_made"), sem("cleared")
        lam_act, const_made, keywT_made, keyw_moved = sem("lam_act"), sem("const_made"), sem("keywT_made"), sem("keyw_moved")
        cent_made, sq_made, var_made, sd_made = sem("cent_made"), sem("sq_made"), sem("var_made"), sem("sd_made")
        xn_made, kn_made = sem("xn_made"), sem("kn_made")
        xnT_ps, xnT_made = sem("xnT_ps"), sem("xnT_made")
        kT_ps, kT_made = sem("kT_ps"), sem("kT_made")
        stat_ps, stat_made, y0_made = sem("stat_ps"), sem("stat_made"), sem("y0_made")
        logits_ps, max_made, exp_made, both_made = sem("logits_ps"), sem("max_made"), sem("exp_made"), sem("both_made")
        counts_ps, owner_made, pos_made, scattered = sem("counts_ps"), sem("owner_made"), sem("pos_made"), sem("scattered")
        kp_made, gram_ps, gram_used, gy_made = sem("kp_made"), sem("gram_ps"), sem("gram_used"), sem("gy_made")
        xg_in = [sem(f"xg_in{i}") for i in range(AHEAD)]
        xT_ps, xT_made, wst_made = sem("xT_ps"), sem("xT_made"), sem("wst_made")
        h_ps, h_relu, h_made = sem("h_ps"), sem("h_relu"), sem("h_made")
        y_ps, y_moved = sem("y_ps"), sem("y_moved")
        y_out = [sem(f"y_out{i}") for i in range(2)]
        staged = sem("staged")
        u_ps, u_made, r_ps, r_made = sem("u_ps"), sem("u_made"), sem("r_ps"), sem("r_made")
        sh_ps, sh_relu, sh_made, sy_ps = sem("sh_ps"), sem("sh_relu"), sem("sh_made"), sem("sy_ps")
        fetched = [sem(f"fetched{i}") for i in range(2)]
        ix_made, acc_made, yvar_made, ysd_made, yo_made = sem("ix_made"), sem("acc_made"), sem("yvar_made"), sem("ysd_made"), sem("yo_made")
        out_done = [sem(f"out_done{i}") for i in range(2)]
        dve_c = sem("dve_c")

        def head_col(ap):
            return ap.rearrange("(h o) -> h o", o=1).to_broadcast([H, HD])

        def tile_blocks(t, i):
            return t[:, :, bass.ds(i * (2 * B), 2 * B)].rearrange("p t (b r) -> p b r t", r=2)

        block = ctx.enter_context(nc.Block())

        def solve_and_slots(eng, solve, slot):
            for s in range(TB - 1):
                solve(0, s)
            slot(None, None)
            with eng.Fori(1, QT) as q:
                for s in range(TB - 1):
                    solve(q, s)
                    for j in DUE[s]:
                        slot(q - 1, j)

        @block.sync
        def _(sp):
            for s_ in y_out + out_done:
                sp.sem_inc(s_, 16)
            sp.dma_start(lam_sb[:, :], head_col(lam)).then_inc(head_in, 16)
            sp.dma_start(eta_sb[:, :], head_col(eta)).then_inc(head_in, 16)
            for b in range(B):
                sp.dma_start(xs[b * TS:(b + 1) * TS, :, :],
                             x[b].rearrange("(i q) d -> q i d", q=TS)).then_inc(x_in, 16)
            sp.dma_start(rw_sb[:, :], rwT).then_inc(w_in, 16)
            sp.dma_start(w_sb[:, :], wT).then_inc(w_in, 16)
            sp.dma_start(knw_sb[:, :], knw.rearrange("(o k) -> o k", o=1).to_broadcast([P, HD])).then_inc(const_in, 16)
            sp.dma_start(onw_sb[:, :], onw.rearrange("(o k) -> o k", o=1).to_broadcast([P, D])).then_inc(const_in, 16)
            sp.dma_start(onb_sb[:, :], onb.rearrange("(o k) -> o k", o=1).to_broadcast([P, D])).then_inc(const_in, 16)
            sp.wait_ge(zeros_made, 1)
            zeros = KT[:, :, :].rearrange("p t c -> p (t c)")
            all_slots = slot_x.rearrange("(p r) d -> p (r d)", p=P)
            n = (SLOTS + AHEAD) * D
            for at in range(0, n, NT * D):
                m = min(NT * D, n - at)
                sp.dma_start(all_slots[:, at:at + m], zeros[:, 0:m]).then_inc(cleared, 16)
            sp.dma_start(fc_sb[:, :, :], fcT).then_inc(routed_in, 16)
            sp.dma_start(pj_sb[:, :, :, :], pjT).then_inc(routed_in, 16)
            sp.dma_start(sfc_sb[:, :], sfcT).then_inc(shared_in, 16)
            sp.dma_start(spj_sb[:, :, :], spjT).then_inc(shared_in, 16)

            def load(t, k):
                sp.dma_start(xg[k], slot_x[bass.ds(t * P, P), :]).then_inc(xg_in[k], 16)

            def slot(q, j):
                if q is None:
                    sp.wait_ge(scattered, TOPK * NT * 16)
                    sp.wait_ge(xnT_ps, NT // 4)
                    sp.wait_ge(kn_made, 1)
                    for k in range(AHEAD):
                        load(k, k)
                    return
                t = q * SPQ + j
                sp.wait_ge(xT_ps, t + 1)
                load(t + AHEAD, j % AHEAD)
                sp.wait_ge(y_moved, t + 2)
                sp.dma_start(slot_y[bass.ds(t * P, P), :], ys[j % 2]).then_inc(y_out[j % 2], 16)

            solve_and_slots(sp, lambda q, s: None, slot)
            with sp.Fori(0, NT // 2) as it:
                for u in range(2):
                    sp.wait_ge(yo_made, it * 2 + (u + 1))
                    for b in range(B):
                        sp.dma_start(out[b].rearrange("(i q) d -> i q d", q=TS)[bass.ds(it * 2 + u, 1)].rearrange("o q d -> (o q) d"),
                                     yo[u][b * TS:(b + 1) * TS, :]).then_inc(out_done[u], 16)
            for u in range(2):
                sp.wait_ge(out_done[u], 16 + NT // 2 * B * 16)
                sp.wait_ge(y_out[u], 16 + SLOTS // 2 * 16)
            for k in range(AHEAD):
                sp.wait_ge(xg_in[k], (SLOTS // AHEAD + 1) * 16)

        @block.gpsimd
        def _(pool):
            g = nc.gpsimd
            g.memset(KT[:, :, :], 0.0).then_inc(zeros_made, 1)
            m = Count(masks_made)
            m.up(g.memset(ident[:, :], 0.0))
            m.up(g.memset(same[:, :], 1.0))
            m.up(g.memset(before[:, :], 1.0))
            m.up(g.memset(ones[:, :], 1.0))
            pool.wait_ge(masks_made, m.n)
            m.up(g.affine_select(out=ident[:, :], in_=ident[:, :], compare_op=ALU.not_equal, fill=1.0,
                                 base=0, pattern=[[-1, P]], channel_multiplier=1))
            m.up(g.affine_select(out=before[:, :], in_=before[:, :], compare_op=ALU.is_ge, fill=0.0,
                                 base=-1, pattern=[[1, P]], channel_multiplier=-1))
            sv = same[:, :].rearrange("p (h k) -> p h k", k=HD)
            m.up(g.affine_select(out=sv, in_=sv, compare_op=ALU.is_ge, fill=0.0,
                                 base=0, pattern=[[-HD, H], [0, HD]], channel_multiplier=1))
            pool.wait_ge(masks_made, m.n)
            m.up(g.affine_select(out=sv, in_=sv, compare_op=ALU.is_ge, fill=0.0,
                                 base=HD - 1, pattern=[[HD, H], [0, HD]], channel_multiplier=-1))
            assert m.n == MASKS
            g.iota(rank[:, :], pattern=[[-1, E]], base=E, channel_multiplier=0,
                   allow_small_or_imprecise_dtypes=True).then_inc(iotas_made, 1)
            g.iota(steps[:, :], pattern=[[P, NT]], base=0, channel_multiplier=0,
                   allow_small_or_imprecise_dtypes=True).then_inc(iotas_made, 1)
            g.iota(slot_no, pattern=[[1, SLOTS + AHEAD]], base=0, channel_multiplier=0,
                   allow_small_or_imprecise_dtypes=True).then_inc(iotas_made, 1)
            g.memset(R[:, :, :], 0.0).then_inc(r_made, 1)

            pool.wait_ge(cleared, CLEARS * 16)
            pool.wait_ge(xn_made, 1)
            pool.wait_ge(pos_made, 1)
            for i in range(NT):
                for k in range(TOPK):
                    g.indirect_dma_start(out=slot_x, out_offset=bass.IndirectOffsetOnAxis(ap=pos[:, i, k:k + 1], axis=0),
                                         in_=xn[:, i, :], in_offset=None).then_inc(scattered, 16)

            def solve(q, s):
                step = q * (TB - 1) + s
                n = TB - 1 - s
                cols = bass.ds(q * QB, QB)
                pool.wait_ge(gram_ps, (step if s == 0 else step - 1) + 1)
                g.tensor_tensor(KP[s % 2][:, 0:n, :], KT[:, s + 1:TB, cols],
                                KT[:, s:s + 1, cols].to_broadcast([P, n, QB]), ALU.mult).then_inc(kp_made, 1)

            def stage_weights(t, k):
                e = pool.value_load(owner[0:1, bass.ds(t, 1)], min_val=0, max_val=E - 1)
                g.tensor_copy(wst[k], fc_sb[:, bass.ds(e, 1), :].rearrange("p o f -> p (o f)")).then_inc(wst_made, 1)

            def slot(q, j):
                if q is None:
                    pool.wait_ge(owner_made, 1)
                    pool.wait_ge(routed_in, 32)
                    pool.wait_ge(scattered, TOPK * NT * 16)
                    pool.wait_ge(xnT_ps, NT // 4)
                    pool.wait_ge(kn_made, 1)
                    for k in range(2):
                        stage_weights(k, k)
                    return
                t = q * SPQ + j
                pool.wait_ge(h_ps, t + 1)
                stage_weights(t + 2, j % 2)

            pool.wait_ge(kT_made, NT // 4)
            solve_and_slots(pool, solve, slot)

            def stage(i, u):
                g.tensor_copy(ix[u][:, :], pos[:, bass.ds(i, 1), :].rearrange("p o k -> p (o k)")).then_inc(ix_made, 1)
                g.tensor_copy(GS[u].rearrange("p (b r t) -> p b r t", b=B, r=2),
                              tile_blocks(GY[:, :, 0, :], i)).then_inc(staged, 1)
                for r in range(2):
                    g.tensor_copy(YS[u][:, r, :].rearrange("p (b r t) -> p b r t", b=B, r=2)[:, :, r, :],
                                  tile_blocks(GY[:, :, 1, :], i)[:, :, r, :]).then_inc(staged, 1)
                pool.wait_ge(ix_made, i + 3)
                g.tensor_tensor(KS[u], kn[:, bass.ds(i, 1), :].to_broadcast([P, 2, D]),
                                keyw[:, 0:2, :], ALU.mult).then_inc(staged, 1)
                for k in range(TOPK):
                    g.indirect_dma_start(out=gy[u][k][:, :], out_offset=None, in_=slot_y,
                                         in_offset=bass.IndirectOffsetOnAxis(ap=ix[u][:, k:k + 1], axis=0)).then_inc(fetched[u], 16)

            for u in range(2):
                pool.wait_ge(y_out[u], 16 + SLOTS // 2 * 16)
            pool.wait_ge(gy_made, QT * (TB - 1))
            pool.wait_ge(keyw_moved, 3)
            for u in range(2):
                g.memset(YS[u], 0.0).then_inc(ix_made, 1)
            pool.wait_ge(ix_made, 2)
            for u in range(2):
                stage(u, u)
            with pool.Fori(0, NT // 2 - 1) as it:
                for u in range(2):
                    i = it * 2 + u
                    pool.wait_ge(r_made, i * 2 + 3)
                    pool.wait_ge(acc_made, i + 1)
                    stage(i + 2, u)

        @block.scalar
        def _(act):
            for s_ in (h_made, y_moved):
                act.sem_inc(s_, 1)
            act.wait_ge(head_in, 32)
            nc.scalar.activation(small[:, 0:1], lam_sb[:, :], ACT.Exp, scale=-1.0).then_inc(lam_act, 1)
            nc.scalar.activation(small[:, 1:2], eta_sb[:, :], ACT.Tanh).then_inc(lam_act, 1)
            act.wait_ge(cent_made, 1)
            nc.scalar.activation(tmp[:, :], flat(xn[:, :, :]), ACT.Square).then_inc(sq_made, 1)
            act.wait_ge(var_made, 1)
            nc.scalar.activation(st[:, 2, :], st[:, 1, :], ACT.Sqrt).then_inc(sd_made, 1)
            for g in range(NT // 4):
                act.wait_ge(xnT_ps, g + 1)
                nc.scalar.copy(flat(xnT[:, 4 * g:4 * g + 4, :]), pst[g % 2]).then_inc(xnT_made, 1)
            nc.scalar.activation(tmp[:, :], flat(xn[:, :, :]), ACT.Square).then_inc(sq_made, 1)
            act.wait_ge(var_made, 2)
            nc.scalar.activation(ks[:, 1, :], ks[:, 0, :], ACT.Sqrt).then_inc(sd_made, 1)
            act.wait_ge(max_made, 1)
            nc.scalar.activation(pb, pr, ACT.Exp).then_inc(exp_made, 1)
            for g in range(NT // 4):
                act.wait_ge(kT_ps, g + 1)
                if g == 0:
                    act.wait_ge(cleared, CLEARS * 16)
                nc.scalar.copy(KT[:, :, 32 * g:32 * g + 32].rearrange("p t c -> p c t"),
                               pst[2 + g % 2].rearrange("p (c t) -> p c t", t=TB)).then_inc(kT_made, 1)
            act.wait_ge(kn_made, 1)
            nc.scalar.activation(tmp[:, :], flat(kn[:, :, :]), ACT.Square).then_inc(sq_made, 1)
            for g in range(NT // 4):
                act.wait_ge(stat_ps, g + 1)
                nc.scalar.copy(GY[:, :, 0, 32 * g:32 * g + 32].rearrange("p t c -> p c t"),
                               pst[g % 2].rearrange("p (c t) -> p c t", t=TB)).then_inc(stat_made, 1)
            act.wait_ge(const_made, CONSTS)
            act.wait_ge(kT_made, NT // 4)
            for t in range(TB):
                nc.scalar.activation(GY[:, t, 1, :], KT[:, t, :], ACT.Copy, scale=powr[:, t + 1:t + 2]).then_inc(y0_made, 1)

            def to_T(t, k):
                nc.scalar.copy(xT[k], psX).then_inc(xT_made, 1)

            def hidden(t, k):
                nc.scalar.activation(hr[k], psH[k], ACT.Relu).then_inc(h_relu, 1)
                act.wait_ge(h_relu, t + 1)
                nc.scalar.activation(hs[k], hr[k], ACT.Square).then_inc(h_made, 1)

            def slot(q, j):
                if q is None:
                    for k in range(2):
                        act.wait_ge(xT_ps, k + 1)
                        to_T(k, k)
                    act.wait_ge(h_ps, 1)
                    hidden(0, 0)
                    return
                t = q * SPQ + j
                act.wait_ge(xT_ps, t + 3)
                act.wait_ge(h_ps, t + 1)
                to_T(t + 2, j % 2)
                act.wait_ge(h_ps, t + 2)
                act.wait_ge(h_made, t + 1)
                act.wait_ge(y_ps, t + 1)
                hidden(t + 1, (j + 1) % 2)
                act.wait_ge(y_ps, t + 2)
                act.wait_ge(y_out[j % 2], q * (SPQ // 2 * 16) + (j // 2 * 16 + 16))
                nc.scalar.copy(ys[j % 2], psY).then_inc(y_moved, 1)

            solve_and_slots(act, lambda q, s: None, slot)

            with act.Fori(0, NT // 2) as it:
                for u in range(2):
                    i = it * 2 + u
                    act.wait_ge(u_ps, i * 2 + 1)
                    nc.scalar.copy(U[u][:, 0, :], psU).then_inc(u_made, 1)
                    act.wait_ge(sh_ps, i + 1)
                    nc.scalar.activation(hr[0], psH[0], ACT.Relu).then_inc(sh_relu, 1)
                    act.wait_ge(sh_relu, i + 1)
                    nc.scalar.activation(hs[0], hr[0], ACT.Square).then_inc(sh_made, 1)
                    act.wait_ge(u_ps, i * 2 + 2)
                    nc.scalar.copy(U[u][:, 1, :], psU).then_inc(u_made, 1)
                    act.wait_ge(yvar_made, i + 1)
                    nc.scalar.activation(ysd[:, :], ymv[:, 2:3], ACT.Sqrt).then_inc(ysd_made, 1)

        @block.vector
        def _(dve):
            c = Count(dve_c)

            def link(ins):
                dve.wait_ge(dve_c, c.up(ins))

            v = nc.vector
            q_ = Count(const_made)

            def qlink(ins):
                dve.wait_ge(const_made, q_.up(ins))

            dve.wait_ge(masks_made, MASKS)
            dve.wait_ge(lam_act, 2)
            qlink(v.tensor_scalar(small[:, 2:3], small[:, 0:1], 1.0, None, ALU.add))
            q_.up(v.memset(powr[:, 0:1], 1.0))
            qlink(v.reciprocal(powr[:, 1:2], small[:, 2:3]))
            qlink(v.tensor_scalar(small[:, 3:4], powr[:, 1:2], -1.0, 1.0, ALU.mult, ALU.add))
            qlink(v.tensor_scalar(small[:, 4:5], small[:, 3:4], small[:, 1:2], 1.0 / HD, ALU.mult, ALU.mult))
            n = 1
            while n < TB:
                qlink(v.tensor_scalar(powr[:, n + 1:2 * n + 1], powr[:, 1:n + 1], powr[:, n:n + 1], None, ALU.mult))
                n *= 2
            qlink(v.tensor_scalar(cpow[:, :], powr[:, :], small[:, 4:5], None, ALU.mult))
            q_.up(v.tensor_scalar(decay[:, :], ident[:, :], powr[:, TB:TB + 1], None, ALU.mult))
            for t in range(TB):
                q_.up(v.tensor_copy(keywT[:, 0, :].rearrange("p (a t) -> p a t", t=TB)[:, :, t:t + 1],
                                    cpow[:, TB - 1 - t:TB - t].unsqueeze(1).to_broadcast([P, P // TB, 1])))
            q_.up(v.tensor_copy(keywT[:, 1, :], small[:, 4:5].to_broadcast([P, P])))
            q_.up(v.tensor_tensor(headsum[:, :, :], same[:, :].unsqueeze(1).to_broadcast([P, TB, P]),
                                  cpow[:, 0:TB].unsqueeze(2).to_broadcast([P, TB, P]), ALU.mult))
            assert q_.n == CONSTS, q_.n

            dve.wait_ge(x_in, 64)
            link(v.tensor_reduce(st[:, 0, :], xs[:, :, :], AX.X, ALU.add))
            link(v.tensor_scalar(st[:, 3, :], st[:, 0, :], 1.0 / D, None, ALU.mult))
            v.tensor_tensor(xn[:, :, :], xs[:, :, :], st[:, 3, :].unsqueeze(2).to_broadcast([P, NT, D]),
                            ALU.subtract).then_inc(cent_made, 1)
            dve.wait_ge(sq_made, 1)
            link(v.tensor_reduce(st[:, 0, :], tmp[:, :].rearrange("p (i d) -> p i d", d=D), AX.X, ALU.add))
            v.tensor_scalar(st[:, 1, :], st[:, 0, :], 1.0 / D, LN_EPS, ALU.mult, ALU.add).then_inc(var_made, 1)
            dve.wait_ge(sd_made, 1)
            link(v.reciprocal(st[:, 3, :], st[:, 2, :]))
            dve.wait_ge(cent_made, 1)
            v.tensor_tensor(xn[:, :, :], xn[:, :, :], st[:, 3, :].unsqueeze(2).to_broadcast([P, NT, D]),
                            ALU.mult).then_inc(xn_made, 1)
            dve.wait_ge(const_in, 3 * 16)
            dve.wait_ge(xn_made, 1)
            link(v.tensor_tensor(xs[:, :, :], xs[:, :, :], onb_sb[:, :].unsqueeze(1).to_broadcast([P, NT, D]), ALU.add))
            dve.wait_ge(sq_made, 2)
            link(v.tensor_reduce(ks[:, 1, :], tmp[:, :].rearrange("p (i k) -> p i k", k=HD), AX.X, ALU.add))
            v.tensor_scalar(ks[:, 0, :], ks[:, 1, :], 1.0 / HD, RMS_EPS, ALU.mult, ALU.add).then_inc(var_made, 1)

            def over_e(ap):
                return ap.unsqueeze(2).to_broadcast([P, NT, E])

            def by_e(ap):
                return ap.rearrange("p (i e) -> p i e", e=E)

            dve.wait_ge(logits_ps, 1)
            lg = by_e(pslog)
            link(v.tensor_reduce(st[:, 0, :], lg, AX.X, ALU.max))
            v.tensor_tensor(pr, lg, over_e(st[:, 0, :]), ALU.subtract).then_inc(max_made, 1)
            dve.wait_ge(exp_made, 1)
            link(v.tensor_reduce(st[:, 0, :], pb, AX.X, ALU.add))
            link(v.reciprocal(st[:, 1, :], st[:, 0, :]))
            link(v.tensor_tensor(pr, pb, over_e(st[:, 1, :]), ALU.mult))
            dve.wait_ge(iotas_made, 3)
            rankb = rank[:, :].unsqueeze(1).to_broadcast([P, NT, E])
            for k in range(TOPK):
                link(v.tensor_reduce(wgt[:, k, :], pr, AX.X, ALU.max))
                link(v.tensor_tensor(pb, pr, over_e(wgt[:, k, :]), ALU.is_equal))
                link(v.tensor_tensor(pb, pb, rankb, ALU.mult))
                link(v.tensor_reduce(st[:, 2, :], pb, AX.X, ALU.max))
                link(v.tensor_tensor(pick[k], pb, over_e(st[:, 2, :]), ALU.is_equal))
                if k == 0:
                    link(v.scalar_tensor_tensor(pr, pick[0], -2.0, pr, ALU.mult, ALU.add))
            v.tensor_tensor(both, pick[0], pick[1], ALU.add).then_inc(both_made, 1)
            link(v.tensor_tensor(st[:, 2, :], wgt[:, 0, :], wgt[:, 1, :], ALU.add))
            link(v.tensor_scalar(st[:, 2, :], st[:, 2, :], 1e-9, None, ALU.max))
            link(v.reciprocal(st[:, 3, :], st[:, 2, :]))
            link(v.tensor_tensor(wgt[:, :, :], wgt[:, :, :], st[:, 3:4, :].to_broadcast([P, TOPK, NT]), ALU.mult))
            dve.wait_ge(counts_ps, 1)
            link(v.tensor_copy(total, by_e(pstotal)))
            for e in range(E):
                c.up(v.tensor_tensor_scan(upto[:, e, :], ones[:, 0:NT], total[:, :, e], 0.0, ALU.mult, ALU.add))
            dve.wait_ge(dve_c, c.n)
            link(v.tensor_tensor(need, upto[:, :, NT - 1:NT].to_broadcast([P, E, NT]),
                                 steps[:, :].unsqueeze(1).to_broadcast([P, E, NT]), ALU.is_gt))
            link(v.tensor_reduce(tiles[:, 0, :], need, AX.X, ALU.add))
            link(v.tensor_tensor_scan(tiles[:, 1, :], ones[:, 0:E], tiles[:, 0, :], 0.0, ALU.mult, ALU.add))
            link(v.tensor_tensor(tiles[:, 2, :], tiles[:, 1, :], tiles[:, 0, :], ALU.subtract))
            uptov = upto.rearrange("p e i -> p i e")
            link(v.tensor_tensor(pb, uptov, total, ALU.subtract))
            link(v.tensor_tensor(pb, pb, by_e(psbefore), ALU.add))
            link(v.scalar_tensor_tensor(pb, tiles[:, 2:3, :].to_broadcast([P, NT, E]), float(P), pb,
                                        ALU.mult, ALU.add))
            for k in range(TOPK):
                link(v.tensor_tensor(pr, pick[k], pb, ALU.mult))
                link(v.tensor_reduce(pos_f[:, :, k:k + 1], pr, AX.X, ALU.add))
            v.tensor_copy(pos[:, :, :], pos_f).then_inc(pos_made, 1)
            nsl = SLOTS + AHEAD
            link(v.tensor_tensor(past, slot_no.unsqueeze(2).to_broadcast([P, nsl, E]),
                                 tiles[:, 1:2, :].to_broadcast([P, nsl, E]), ALU.is_ge))
            link(v.tensor_reduce(owner_f, past, AX.X, ALU.add))
            link(v.tensor_scalar(owner_f, owner_f, float(E - 1), None, ALU.min))
            v.tensor_copy(owner[:, :], owner_f).then_inc(owner_made, 1)

            dve.wait_ge(sd_made, 2)
            link(v.reciprocal(ks[:, 0, :], ks[:, 1, :]))
            knv = kn[:, :, :].rearrange("p i (h k) -> p (i h) k", k=HD)
            link(v.tensor_tensor(knv, xn[:, :, :].rearrange("p i (h k) -> p (i h) k", k=HD),
                                 ks[:, 0, :].unsqueeze(2).to_broadcast([P, NT * H, HD]), ALU.mult))
            v.tensor_tensor(knv, knv, knw_sb[:, :].unsqueeze(1).to_broadcast([P, NT * H, HD]),
                            ALU.mult).then_inc(kn_made, 1)
            dve.wait_ge(keywT_made, 1)
            k3 = Count(keyw_moved)
            link(v.tensor_reduce(half[:, 0:1], ident[:, :].rearrange("p (b r t) -> p b r t", b=B, r=2)[:, :, 0, :],
                                 AX.XY, ALU.add))
            link(v.tensor_scalar(half[:, 1:2], half[:, 0:1], -1.0, 1.0, ALU.mult, ALU.add))
            for r in range(2):
                k3.up(v.tensor_scalar(keyw[:, r, :], pskw[:, 0:P], half[:, r:r + 1], None, ALU.mult))
            k3.up(v.tensor_copy(keyw[:, 2, :], pskw[:, P:2 * P]))
            dve.wait_ge(keyw_moved, 3)
            dve.wait_ge(sq_made, 3)
            link(v.tensor_reduce(ks[:, 0, :], tmp[:, :].rearrange("p (i k) -> p i k", k=HD), AX.X, ALU.add))
            link(v.tensor_tensor(fac[:, :, :], ks[:, 0, :].rearrange("p (i h) -> p i h", h=H),
                                 keyw[:, 2, :].rearrange("p (h k) -> p k h", k=HD)[:, 0:1, :]
                                 .to_broadcast([P, NT, H]), ALU.mult))
            link(v.tensor_scalar(fac[:, :, :], fac[:, :, :], 1.0, None, ALU.add))

            dve.wait_ge(stat_made, NT // 4)
            dve.wait_ge(y0_made, TB)
            dve.sem_inc(gy_made, 1)
            prod = tmp[:, 0:(TB - 1) * 2 * QB].rearrange("p (t g c) -> p t g c", g=2, c=QB)

            def solve(q, s):
                n = TB - 1 - s
                step = q * (TB - 1) + s
                cols = bass.ds(q * QB, QB)
                dve.wait_ge(gram_ps, step + 2)
                dve.wait_ge(gy_made, step + 1)
                gram = ps[s % 2][:, 0:n * QB].rearrange("p (t o c) -> p t o c", o=1, c=QB)
                v.tensor_tensor(prod[:, 0:n], gram.to_broadcast([P, n, 2, QB]),
                                GY[:, s:s + 1, :, cols].to_broadcast([P, n, 2, QB]), ALU.mult).then_inc(gram_used, 1)
                dve.wait_ge(gram_used, step + 1)
                v.tensor_tensor(GY[:, s + 1:TB, :, cols], GY[:, s + 1:TB, :, cols], prod[:, 0:n],
                                ALU.add).then_inc(gy_made, 1)

            solve_and_slots(dve, solve, lambda q, j: None)

            base = c.n
            with dve.Fori(0, NT // 2) as it:
                c.n = 0

                def llink(ins):
                    dve.wait_ge(dve_c, it * LINKS + (base + c.up(ins)))

                for u in range(2):
                    i = it * 2 + u

                    def mask_state(r):
                        dve.wait_ge(r_ps, i * 2 + (r + 1))
                        for n in range(2):
                            ins = v.tensor_tensor(R[:, 2 * n:2 * n + 2, :], psRv[n],
                                                  same[:, :].unsqueeze(1).to_broadcast([P, 2, D]), ALU.mult)
                        ins.then_inc(r_made, 1)

                    def tile_of(t3):
                        return t3[:, bass.ds(i, 1), :].rearrange("p o d -> p (o d)")

                    mask_state(0)
                    dve.wait_ge(sy_ps, i + 1)
                    llink(v.tensor_tensor(acc, psY, tile_of(xs), ALU.add))
                    dve.wait_ge(fetched[u], it * (TOPK * 16) + TOPK * 16)
                    llink(v.scalar_tensor_tensor(acc, gy[u][0][:, :], wgt[:, 0, bass.ds(i, 1)], acc, ALU.mult, ALU.add))
                    mask_state(1)
                    dve.wait_ge(u_made, i * 2 + 2)
                    ybv = yb.rearrange("p (h k) -> p h k", k=HD)
                    llink(v.tensor_tensor(ybv, U[u][:, 1, :].rearrange("p (h k) -> p h k", k=HD),
                                          tile_of(fac).unsqueeze(2).to_broadcast([P, H, HD]), ALU.mult))
                    llink(v.bn_stats(yst[:, :], yb))
                    v.scalar_tensor_tensor(acc, gy[u][1][:, :], wgt[:, 1, bass.ds(i, 1)], acc,
                                           ALU.mult, ALU.add).then_inc(acc_made, 1)
                    llink(v.bn_aggr(ymv[:, 0:2], yst[:, :]))
                    v.tensor_scalar(ymv[:, 2:3], ymv[:, 1:2], LN_EPS, None, ALU.add).then_inc(yvar_made, 1)
                    dve.wait_ge(ysd_made, i + 1)
                    llink(v.reciprocal(ymv[:, 3:4], ysd[:, :]))
                    llink(v.tensor_scalar(yb, yb, ymv[:, 0:1], ymv[:, 3:4], ALU.subtract, ALU.mult))
                    llink(v.tensor_tensor(yb, yb, onw_sb[:, :], ALU.mult))
                    dve.wait_ge(acc_made, i + 1)
                    dve.wait_ge(out_done[u], it * (B * 16) + 16)
                    v.tensor_tensor(yo[u], yb, acc, ALU.add).then_inc(yo_made, 1)
                    dve.wait_ge(yo_made, i + 1)
                assert c.n == LINKS, c.n

        @block.tensor
        def _(pe):
            mm, tr = nc.tensor.matmul, nc.tensor.transpose
            for s_ in (gram_ps, y_ps):
                pe.sem_inc(s_, 1)
            pe.wait_ge(masks_made, MASKS)
            pe.wait_ge(xn_made, 1)
            for g in range(NT // 4):
                if g >= 2:
                    pe.wait_ge(xnT_made, g - 1)
                for j in range(4):
                    ins = tr(pst[g % 2][:, P * j:P * j + P], xn[:, 4 * g + j, :], ident[:, :])
                ins.then_inc(xnT_ps, 1)
            pe.wait_ge(w_in, 32)
            for i in range(NT):
                if i % 4 == 0:
                    pe.wait_ge(xnT_made, i // 4 + 1)
                ins = mm(pslog[:, E * i:E * i + E], xnT[:, i, :], rw_sb[:, :], start=True, stop=True)
            ins.then_inc(logits_ps, 1)
            pe.wait_ge(const_made, CONSTS)
            tr(pskw[:, 0:P], keywT[:, 0, :], ident[:, :])
            tr(pskw[:, P:2 * P], keywT[:, 1, :], ident[:, :]).then_inc(keywT_made, 1)
            def static(g):
                pe.wait_ge(xnT_made, NT // 4)
                if g >= 2:
                    pe.wait_ge(stat_made, g - 1)
                mm(pst[g % 2], w_sb[:, :], flat(xnT[:, 4 * g:4 * g + 4, :]), start=True, stop=True).then_inc(stat_ps, 1)

            static(0)
            static(1)
            pe.wait_ge(both_made, 1)
            mm(psbefore, before[:, :], flat(both), start=True, stop=True)
            mm(pstotal, ones[:, :], flat(both), start=True, stop=True).then_inc(counts_ps, 1)
            pe.wait_ge(kn_made, 1)
            for g in range(NT // 4):
                if g >= 2:
                    pe.wait_ge(kT_made, g - 1)
                for j in range(4):
                    ins = tr(pst[2 + g % 2][:, P * j:P * j + P], kn[:, 4 * g + j, :], ident[:, :])
                ins.then_inc(kT_ps, 1)
            for g in range(2, NT // 4):
                static(g)
            pe.wait_ge(stat_made, NT // 4)

            def solve(q, s):
                n = TB - 1 - s
                step = q * (TB - 1) + s
                pe.wait_ge(kp_made, step + 1)
                if s == 0:
                    if not isinstance(q, int):
                        pe.wait_ge(gram_used, step)
                elif not (isinstance(q, int) and step < 2):
                    pe.wait_ge(gram_used, step - 1)
                for t in range(n):
                    ins = mm(ps[s % 2][:, t * QB:(t + 1) * QB], headsum[:, t + 1, :], KP[s % 2][:, t, :],
                             start=True, stop=True)
                ins.then_inc(gram_ps, 1)

            def to_T(t, k):
                tr(psX, xg[k], ident[:, :]).then_inc(xT_ps, 1)

            def up(t, k):
                for f in range(FC):
                    ins = mm(psH[k][:, f * P:f * P + P], wst[k][:, f * P:f * P + P], xT[k], start=True, stop=True)
                ins.then_inc(h_ps, 1)

            def slot(q, j):
                if q is None:
                    pe.wait_ge(owner_made, 1)
                    pe.wait_ge(routed_in, 32)
                    pe.wait_ge(keyw_moved, 3)
                    for k in range(2):
                        pe.wait_ge(xg_in[k], 16)
                        if k:
                            pe.wait_ge(xT_made, k)
                        to_T(k, k)
                    pe.wait_ge(xT_made, 1)
                    pe.wait_ge(wst_made, 1)
                    up(0, 0)
                    return
                t = q * SPQ + j
                pe.wait_ge(xg_in[(j + 2) % AHEAD], q * (SPQ // AHEAD * 16) + ((j + 2) // AHEAD * 16 + 16))
                pe.wait_ge(xT_made, t + 2)
                to_T(t + 2, (j + 2) % AHEAD)
                pe.wait_ge(wst_made, t + 2)
                pe.wait_ge(h_relu, t + 1)
                up(t + 1, (j + 1) % 2)
                e = pe.value_load(owner[0:1, bass.ds(t, 1)], min_val=0, max_val=E - 1)
                pe.wait_ge(h_made, t + 2)
                pe.wait_ge(y_moved, t + 1)
                for f in range(FC):
                    ins = mm(psY, hs[j % 2][:, f * P:f * P + P],
                             pj_sb[:, bass.ds(e, 1), f, :].rearrange("p o d -> p (o d)"), start=(f == 0), stop=(f == FC - 1))
                ins.then_inc(y_ps, 1)

            solve_and_slots(pe, solve, slot)

            pe.wait_ge(shared_in, 32)
            pe.wait_ge(gram_used, QT * (TB - 1))
            pe.wait_ge(h_made, SLOTS + 2)
            pe.wait_ge(y_moved, SLOTS + 1)
            with pe.Fori(0, NT // 2) as it:
                for u in range(2):
                    i = it * 2 + u
                    pe.wait_ge(staged, i * 4 + 4)
                    mm(psU, GS[u], ident[:, :], start=True, stop=False, skip_group_check=True)
                    for r in range(2):
                        pe.wait_ge(r_made, i * 2 + (r + 1))
                        for b in range(B):
                            ins = mm(psU[b * TS:(b + 1) * TS, :], YS[u][:, r, b * TS:(b + 1) * TS], R[:, b, :],
                                     start=False, stop=True, skip_group_check=True)
                        ins.then_inc(u_ps, 1)
                        for b in range(B):
                            mm(psR[b], decay[:, :], R[:, b, :], start=True, stop=False)
                        if r == 0:
                            for f in range(FC):
                                ins = mm(psH[0][:, f * P:f * P + P], sfc_sb[:, f * P:f * P + P],
                                         xnT[:, bass.ds(i, 1), :].rearrange("p o t -> p (o t)"), start=True, stop=True)
                            ins.then_inc(sh_ps, 1)
                        pe.wait_ge(u_made, i * 2 + (r + 1))
                        for b in range(B):
                            rows = slice(b * TS, (b + 1) * TS)
                            ins = mm(psR[b], KS[u][rows, r, :], U[u][rows, r, :], start=False, stop=True)
                        ins.then_inc(r_ps, 1)
                        if r == 0:
                            pe.wait_ge(sh_made, i + 1)
                            for f in range(FC):
                                ins = mm(psY, hs[0][:, f * P:f * P + P], spj_sb[:, f, :],
                                         start=(f == 0), stop=(f == FC - 1))
                            ins.then_inc(sy_ps, 1)


MASKS = 8
CONSTS = 1 + 1 + 3 + 4 + 1 + 1 + TB + 1 + 1
CLEARS = -(-(SLOTS + AHEAD) // NT)
LINKS = 2 * 8


def kernel(L0_attn_x, L0_attn_W, L0_attn_k_norm_w, L0_attn_o_norm_w, L0_attn_o_norm_b, L0_attn_eta_raw,
           L0_attn_lam_logit, L0_ffn_router_w, L0_ffn_w_fc, L0_ffn_w_proj, L0_ffn_shared_fc, L0_ffn_shared_proj):
    import concourse.bacc as bacc
    from concourse.bass_utils import run_bass_kernel_spmd

    def lay(a, order=None, shape=None):
        a = np.asarray(a)
        if shape:
            a = a.reshape(shape)
        return np.ascontiguousarray(a.transpose(order) if order else a)

    ins = {
        "x": lay(L0_attn_x),
        "wT": lay(L0_attn_W, (1, 0)),
        "knw": lay(L0_attn_k_norm_w), "onw": lay(L0_attn_o_norm_w), "onb": lay(L0_attn_o_norm_b),
        "eta": lay(L0_attn_eta_raw), "lam": lay(L0_attn_lam_logit),
        "rwT": lay(L0_ffn_router_w, (1, 0)),
        "fcT": lay(L0_ffn_w_fc, (2, 0, 1)),
        "pjT": lay(L0_ffn_w_proj, (3, 0, 2, 1), (E, D, FC, P)),
        "sfcT": lay(L0_ffn_shared_fc, (1, 0)),
        "spjT": lay(L0_ffn_shared_proj, (2, 1, 0), (D, FC, P)),
    }
    nc = bacc.Bacc("TRN2", target_bir_lowering=False, num_devices=1)
    aps = [nc.dram_tensor(n, a.shape, mybir.dt.from_np(a.dtype), kind="ExternalInput").ap() for n, a in ins.items()]
    out = nc.dram_tensor("out", (B, L, D), F32, kind="ExternalOutput").ap()
    build(nc, *aps, out)
    r = run_bass_kernel_spmd(nc, [ins], core_ids=[0])
    return r.results[0]["out"]
```

```python
import numpy as np

import concourse.bass as bass
import concourse.mybir as mybir

F32 = mybir.dt.float32
I32 = mybir.dt.int32
U32 = mybir.dt.uint32
ALU = mybir.AluOpType
ACT = mybir.ActivationFunctionType
AX = mybir.AxisListType

P = 128
B, L, D, H = 4, 1024, 128, 16
HD = D // H
E, FF = 8, 512
TOPK = 2
FC = FF // P
TB = 16
TS = 2 * TB
NT = L // TS
NB = NT * B * 2
QT = 4
QB = NB // QT
SLOTS = TOPK * NT + E
AHEAD = 4
HG = 4
GW = D // HG
SPQ = [24, 24, 24]
FACT = 4
LN_EPS = 1e-5
RMS_EPS = float(np.finfo(np.float32).eps)


def due(n):
    work = [sum(TB - 1 - j for j in range(k + 1)) for k in range(TB - 1)]
    upto = [round(n * w / work[-1]) for w in work]
    upto = [0] + upto[:-2] + [n]
    return [range(lo, hi) for lo, hi in zip([0] + upto[:-1], upto)]


assert sum(SPQ) == SLOTS and all(n % AHEAD == 0 for n in SPQ) and SPQ[1] == SPQ[2]


class Count:

    def __init__(self, sem):
        self.sem, self.n = sem, 0

    def up(self, ins):
        ins.then_inc(self.sem, 1)
        self.n += 1
        return self.n


def build(nc, x, wT, knw, onw, onb, eta, lam, rwT, fcT, pjT, sfcT, spjT, out):
    from contextlib import ExitStack
    with ExitStack() as ctx:
        def sb(name, shape, dt=F32):
            return ctx.enter_context(nc.sbuf_tensor(name, shape, dt))

        def sem(name):
            return ctx.enter_context(nc.semaphore(name))

        slot_x = nc.dram_tensor("slot_x", [(SLOTS + AHEAD) * P, D], F32).ap()
        slot_y = nc.dram_tensor("slot_y", [SLOTS * P, D], F32).ap()

        xs = sb("xs", [P, NT, D])
        xn = sb("xn", [P, NT, D])
        kn = sb("kn", [P, NT, D])
        tmp = sb("tmp", [P, NT * D])
        xnT = sb("xnT", [P, NT, P])
        KT = sb("KT", [P, TB, NB])
        GY = sb("GY", [P, TB, 2, NB])
        w_sb = sb("w_sb", [P, D])
        rw_sb = sb("rw_sb", [P, E])
        knw_sb = sb("knw_sb", [P, 1])
        onw_sb = sb("onw_sb", [P, D])
        onb_sb = sb("onb_sb", [P, D])
        eta_sb = sb("eta_sb", [P, 1])
        lam_sb = sb("lam_sb", [P, 1])
        ksq = sb("ksq", [P, NT * P])
        wst = [ksq[:, k * FF:(k + 1) * FF] for k in range(AHEAD)]
        pj_sb = sb("pj_sb", [P, E, FC, D])
        sfc_sb = sb("sfc_sb", [P, FF])
        spj_sb = sb("spj_sb", [P, FC, D])
        ident = sb("ident", [P, P])
        same = sb("same", [P, P])
        before = sb("before", [P, P])
        ones = sb("ones", [P, P])
        headsum = sb("headsum", [P, P])
        decay = sb("decay", [P, P])
        csel = sb("csel", [P, H])
        powr = sb("powr", [P, TB + 1])
        cpow = sb("cpow", [P, TB + 1])
        cpw = sb("cpw", [P, TB])
        small = sb("small", [P, 8])
        keyw = sb("keyw", [P, 2, D])
        keywT = sb("keywT", [P, P])
        half = sb("half", [P, 2])
        st = sb("st", [P, 4, NT])
        bst = sb("bst", [P, NT, 6])
        mv = sb("mv", [P, NT, 2])
        ks = sb("ks", [P, 2, NT * H])
        fac = sb("fac", [P, NT, H])
        rank = sb("rank", [P, E])
        steps = sb("steps", [P, NT])
        tiles = sb("tiles", [P, 4, E])
        owner = sb("owner", [P, SLOTS + AHEAD], I32)
        wgt = sb("wgt", [P, TOPK, NT])
        pos = sb("pos", [P, NT, TOPK], U32)
        KP = [sb(f"KP{i}", [P, TB - 1, QB]) for i in range(2)]
        R = sb("R", [P, B, D])
        yst = sb("yst", [P, 6])
        ymv = sb("ymv", [P, 4])
        ysd = sb("ysd", [P, 1])
        turn = sb("turn", [P, 1])

        at = [0]

        def scratch(*shape):
            n = int(np.prod(shape))
            at[0] += n
            ap = GY[:, :, :, :].rearrange("p t g c -> p (t g c)")[:, at[0] - n:at[0]]
            return ap.rearrange("p (a b) -> p a b", b=shape[1]) if len(shape) == 2 else ap

        pr, pb, both = (scratch(NT, E) for _ in range(3))
        pick = [scratch(NT, E) for _ in range(TOPK)]
        total = scratch(NT, E)
        upto, need = scratch(E, NT), scratch(E, NT)
        slot_no, owner_f = scratch(SLOTS + AHEAD), scratch(SLOTS + AHEAD)
        past = scratch(SLOTS + AHEAD, E)
        pos_f = scratch(NT, TOPK)

        def part(t, n):
            at = [0]

            def take(tiles):
                at[0] += tiles
                assert at[0] <= n
                return t[:, at[0] - tiles:at[0], :]
            return take

        def flat(ap):
            return ap.rearrange("p a b -> p (a b)")

        take = part(xn, NT)
        hr = [flat(take(4)) for _ in range(2)]
        hs = [flat(take(4)) for _ in range(2)]
        xT = [flat(take(1)) for _ in range(2)]
        ys = [flat(take(1)) for _ in range(2)]
        xg = [flat(take(1)) for _ in range(AHEAD)]
        take = part(tmp[:, :].rearrange("p (i d) -> p i d", d=D)[:, NT // 2:NT, :], NT // 2)
        GS = [flat(take(1)) for _ in range(2)]
        YS = [take(2) for _ in range(2)]
        KS = [take(2) for _ in range(2)]
        UX = [sb(f"UX{i}", [P, B, D]) for i in range(2)]
        gy = [[sb(f"gy{i}{k}", [P, D]) for k in range(TOPK)] for i in range(2)]
        acc = flat(take(1))
        yb = [flat(take(1)) for _ in range(2)]
        yo = [flat(take(1)) for _ in range(2)]
        ix = [sb(f"ix{i}", [P, TOPK], U32) for i in range(2)]

        ps = [ctx.enter_context(nc.psum_tensor(f"ps{i}", [P, 4, 512], F32)) for i in range(2)]

        def bank(n):
            return ps[n // 4][:, n % 4, :]

        pst = [bank(n) for n in range(4)]
        pslog = bank(4)[:, 0:NT * E]
        psbefore, pstotal = bank(4)[:, 0:NT * E], bank(4)[:, NT * E:2 * NT * E]
        psfac = bank(4)[:, 0:NT * H]
        pskw = bank(7)[:, 0:P]
        psgram = [ps[0][:, 2 * n:2 * n + 2, :].rearrange("p a c -> p (a c)") for n in range(2)]
        psX, psH, psY = bank(4)[:, 0:P], [bank(5), bank(6)], bank(7)[:, 0:D]
        psU = [bank(n)[:, 0:D] for n in range(2)]
        psR = bank(2)[:, 0:B * GW]
        psSH, psS = bank(5), [bank(6 + n)[:, 0:D] for n in range(2)]

        x_in, const_in = [sem(f"x_in{i}") for i in range(2)], [sem(f"const_in{i}") for i in range(2)]
        w_in, head_in = sem("w_in"), sem("head_in")
        routed_in, shared_in = sem("routed_in"), sem("shared_in")
        masks_made, iotas_made, zeros_made, cleared = sem("masks_made"), sem("iotas_made"), sem("zeros_made"), sem("cleared")
        lam_act, const_made, keywT_made, keyw_moved = sem("lam_act"), sem("const_made"), sem("keywT_made"), sem("keyw_moved")
        stats_made, sq_made, var_made, sd_made = sem("stats_made"), sem("sq_made"), sem("var_made"), sem("sd_made")
        scale_made, xna_made, xs_made = sem("scale_made"), sem("xna_made"), sem("xs_made")
        fac_ps, fac_read = sem("fac_ps"), sem("fac_read")
        xn_made, kn_made = sem("xn_made"), sem("kn_made")
        xnT_ps, xnT_made = sem("xnT_ps"), sem("xnT_made")
        kT_ps, kT_made = sem("kT_ps"), sem("kT_made")
        stat_ps, stat_made = sem("stat_ps"), sem("stat_made")
        logits_ps, max_made, exp_made, both_made = sem("logits_ps"), sem("max_made"), sem("exp_made"), sem("both_made")
        counts_ps, owner_made, pos_made, scattered = sem("counts_ps"), sem("owner_made"), sem("pos_made"), sem("scattered")
        kp_made, gram_ps, gram_used, gy_made = sem("kp_made"), sem("gram_ps"), sem("gram_used"), sem("gy_made")
        xg_in = [sem(f"xg_in{i}") for i in range(AHEAD)]
        xT_ps, xT_made = sem("xT_ps"), sem("xT_made")
        w_fetched = [sem(f"w_fetched{i}") for i in range(AHEAD)]
        h_ps, h_relu, h_made = sem("h_ps"), sem("h_relu"), sem("h_made")
        y_ps, y_moved = sem("y_ps"), sem("y_moved")
        gather_made = sem("gather_made")
        y0_made, headsum_made = sem("y0_made"), sem("headsum_made")
        y_out = [sem(f"y_out{i}") for i in range(2)]
        staged, staged_y = sem("staged"), sem("staged_y")
        u_ps, ua_made, uv_made = sem("u_ps"), sem("ua_made"), sem("uv_made")
        ux_zero, ys_zero = sem("ux_zero"), sem("ys_zero")
        r_ps, r_made, t_read = sem("r_ps"), sem("r_made"), sem("t_read")
        sh_ps, sh_relu, sh_made, sy_ps = sem("sh_ps"), sem("sh_relu"), sem("sh_made"), sem("sy_ps")
        fetched = [sem(f"fetched{i}") for i in range(2)]
        ix_made, acc_made, yvar_made, ysd_made, yo_made = sem("ix_made"), sem("acc_made"), sem("yvar_made"), sem("ysd_made"), sem("yo_made")
        out_done = [sem(f"out_done{i}") for i in range(2)]
        dve_c, pass_c = sem("dve_c"), sem("pass_c")

        def kp_of(s):
            n = TB - 1 - s
            return KP[1][:, 2:3, :] if n == 1 else KP[s % 2][:, 0:n, :]

        def gram_of(s):
            n = TB - 1 - s
            return psgram[1][:, 512:512 + QB] if n == 1 else psgram[s % 2][:, 0:n * QB]

        def head_col(ap):
            return ap.rearrange("(h o) -> h o", o=1).to_broadcast([H, HD])

        def tile_blocks(t, i):
            return t[:, :, bass.ds(i * (2 * B), 2 * B)].rearrange("p t (b r) -> p b r t", r=2)

        block = ctx.enter_context(nc.Block())

        def solve_and_slots(eng, solve, slot):
            for s in range(TB - 1):
                solve(0, s)
            for s, begun in enumerate(due(SPQ[0])):
                solve(1, s)
                if s == 0:
                    slot(None, None)
                for j in begun:
                    slot(0, j)
            with eng.Fori(2, QT) as q:
                for s, begun in enumerate(due(SPQ[1])):
                    solve(q, s)
                    for j in begun:
                        slot(q * SPQ[1] + (SPQ[0] - 2 * SPQ[1]), j)

        @block.sync
        def _(sp):
            for s_ in y_out + out_done:
                sp.sem_inc(s_, 16)
            sp.dma_start(lam_sb[:, :], head_col(lam)).then_inc(head_in, 16)
            sp.dma_start(eta_sb[:, :], head_col(eta)).then_inc(head_in, 16)
            sp.dma_start(knw_sb[:, :], knw.rearrange("(o k) -> o k", o=1).to_broadcast([H, HD])).then_inc(const_in[0], 16)
            for n in range(2):
                for b in range(B):
                    sp.dma_start(xs[b * TS:(b + 1) * TS, n * NT // 2:(n + 1) * NT // 2, :],
                                 x[b, n * L // 2:(n + 1) * L // 2].rearrange("(i q) d -> q i d", q=TS)).then_inc(x_in[n], 16)
            sp.dma_start(rw_sb[:, :], rwT).then_inc(w_in, 16)
            sp.dma_start(w_sb[:, :], wT).then_inc(w_in, 16)
            sp.dma_start(onw_sb[:, :], onw.rearrange("(o k) -> o k", o=1).to_broadcast([P, D])).then_inc(const_in[1], 16)
            sp.dma_start(onb_sb[:, :], onb.rearrange("(o k) -> o k", o=1).to_broadcast([P, D])).then_inc(const_in[1], 16)
            sp.dma_start(sfc_sb[:, :], sfcT).then_inc(shared_in, 16)
            sp.dma_start(spj_sb[:, :, :], spjT).then_inc(shared_in, 16)
            sp.wait_ge(zeros_made, 1)
            zeros = KT[:, :, :].rearrange("p t c -> p (t c)")
            all_slots = slot_x.rearrange("(p r) d -> p (r d)", p=P)
            n = (SLOTS + AHEAD) * D
            for at in range(0, n, NT * D):
                m = min(NT * D, n - at)
                sp.dma_start(all_slots[:, at:at + m], zeros[:, 0:m]).then_inc(cleared, 16)
            sp.dma_start(pj_sb[:, :, :, :], pjT).then_inc(routed_in, 16)

            def load(t, k):
                sp.dma_start(xg[k], slot_x[bass.ds(t * P, P), :]).then_inc(xg_in[k], 16)

            def load_weights(t, k):
                e = sp.value_load(owner[0:1, bass.ds(t, 1)], min_val=0, max_val=E - 1)
                sp.dma_start(wst[k], fcT[:, bass.ds(e, 1), :].rearrange("p o f -> p (o f)")).then_inc(w_fetched[k], 16)

            def slot(t0, j):
                if t0 is None:
                    sp.wait_ge(owner_made, 1)
                    sp.wait_ge(fac_ps, NT // FACT)
                    for k in range(AHEAD):
                        load_weights(k, k)
                    sp.wait_ge(scattered, TOPK * NT * 16)
                    sp.wait_ge(xnT_ps, NT // 4)
                    sp.wait_ge(kn_made, 1)
                    for k in range(AHEAD):
                        load(k, k)
                    return
                t = t0 + j
                sp.wait_ge(xT_ps, t + 1)
                load(t + AHEAD, j % AHEAD)
                sp.wait_ge(h_ps, t + 1)
                load_weights(t + AHEAD, j % AHEAD)
                sp.wait_ge(y_moved, t + 2)
                sp.dma_start(slot_y[bass.ds(t * P, P), :], ys[j % 2]).then_inc(y_out[j % 2], 16)

            solve_and_slots(sp, lambda q, s: None, slot)
            with sp.Fori(0, NT // 2) as it:
                for u in range(2):
                    sp.wait_ge(yo_made, it * 2 + (u + 1))
                    for b in range(B):
                        sp.dma_start(out[b].rearrange("(i q) d -> i q d", q=TS)[bass.ds(it * 2 + u, 1)].rearrange("o q d -> (o q) d"),
                                     yo[u][b * TS:(b + 1) * TS, :]).then_inc(out_done[u], 16)
            for u in range(2):
                sp.wait_ge(out_done[u], 16 + NT // 2 * B * 16)
                sp.wait_ge(y_out[u], 16 + SLOTS // 2 * 16)
            for k in range(AHEAD):
                sp.wait_ge(xg_in[k], (SLOTS // AHEAD + 1) * 16)
                sp.wait_ge(w_fetched[k], (SLOTS // AHEAD + 1) * 16)

        @block.gpsimd
        def _(pool):
            g = nc.gpsimd
            g.memset(KT[:, :, :], 0.0).then_inc(zeros_made, 1)
            m = Count(masks_made)
            m.up(g.memset(ident[:, :], 0.0))
            m.up(g.memset(same[:, :], 1.0))
            m.up(g.memset(before[:, :], 1.0))
            m.up(g.memset(ones[:, :], 1.0))
            pool.wait_ge(masks_made, m.n)
            m.up(g.affine_select(out=ident[:, :], in_=ident[:, :], compare_op=ALU.not_equal, fill=1.0,
                                 base=0, pattern=[[-1, P]], channel_multiplier=1))
            m.up(g.affine_select(out=before[:, :], in_=before[:, :], compare_op=ALU.is_ge, fill=0.0,
                                 base=-1, pattern=[[1, P]], channel_multiplier=-1))
            sv = same[:, :].rearrange("p (h k) -> p h k", k=HD)
            m.up(g.affine_select(out=sv, in_=sv, compare_op=ALU.is_ge, fill=0.0,
                                 base=0, pattern=[[-HD, H], [0, HD]], channel_multiplier=1))
            pool.wait_ge(masks_made, m.n)
            m.up(g.affine_select(out=sv, in_=sv, compare_op=ALU.is_ge, fill=0.0,
                                 base=HD - 1, pattern=[[HD, H], [0, HD]], channel_multiplier=-1))
            assert m.n == MASKS
            g.iota(rank[:, :], pattern=[[-1, E]], base=E, channel_multiplier=0,
                   allow_small_or_imprecise_dtypes=True).then_inc(iotas_made, 1)
            g.iota(steps[:, :], pattern=[[P, NT]], base=0, channel_multiplier=0,
                   allow_small_or_imprecise_dtypes=True).then_inc(iotas_made, 1)
            g.iota(slot_no, pattern=[[1, SLOTS + AHEAD]], base=0, channel_multiplier=0,
                   allow_small_or_imprecise_dtypes=True).then_inc(iotas_made, 1)
            for b in range(2):
                g.memset(R[:, 2 * b:2 * b + 2, :], 0.0).then_inc(r_made, 1)
            for u in range(2):
                g.memset(UX[u][:, :, :], 0.0).then_inc(ux_zero, 1)

            pool.wait_ge(const_in[1], 32)
            pool.wait_ge(xn_made, 2)
            pool.wait_ge(xna_made, 2)
            g.tensor_tensor(xs[:, :, :], xs[:, :, :], onb_sb[:, :].unsqueeze(1).to_broadcast([P, NT, D]),
                            ALU.add).then_inc(xs_made, 1)
            pool.wait_ge(cleared, CLEARS * 16)
            pool.wait_ge(pos_made, 1)
            for i in range(NT):
                for k in range(TOPK):
                    g.indirect_dma_start(out=slot_x, out_offset=bass.IndirectOffsetOnAxis(ap=pos[:, i, k:k + 1], axis=0),
                                         in_=xn[:, i, :], in_offset=None).then_inc(scattered, 16)

            def solve(q, s):
                if isinstance(q, int) and q == 0:
                    return
                step = q * (TB - 1) + s
                n = TB - 1 - s
                cols = bass.ds(q * QB, QB)
                pool.wait_ge(gram_ps, (step - 2 if s == 0 else step - 1) + 1)
                g.tensor_tensor(kp_of(s), KT[:, s + 1:TB, cols],
                                KT[:, s:s + 1, cols].to_broadcast([P, n, QB]), ALU.mult).then_inc(kp_made, 1)

            pool.wait_ge(kp_made, TB - 1)
            solve_and_slots(pool, solve, lambda t0, j: None)

            def stage(i, u):
                g.tensor_copy(ix[u][:, :], pos[:, bass.ds(i, 1), :].rearrange("p o k -> p (o k)")).then_inc(ix_made, 1)
                pool.wait_ge(ix_made, i + 1)
                g.tensor_tensor(KS[u], kn[:, bass.ds(i, 1), :].to_broadcast([P, 2, D]),
                                keyw[:, 0:2, :], ALU.mult).then_inc(staged, 1)

            def fetch(u):
                for k in range(TOPK):
                    g.indirect_dma_start(out=gy[u][k][:, :], out_offset=None, in_=slot_y,
                                         in_offset=bass.IndirectOffsetOnAxis(ap=ix[u][:, k:k + 1], axis=0)).then_inc(fetched[u], 16)

            pool.wait_ge(gy_made, QT * (TB - 1) - 3)
            for u in range(2):
                g.memset(YS[u], 0.0).then_inc(ys_zero, 1)
            for u in range(2):
                stage(u, u)
            for u in range(2):
                pool.wait_ge(y_out[u], 16 + SLOTS // 2 * 16)
            for u in range(2):
                fetch(u)
            with pool.Fori(0, NT // 2 - 1) as it:
                for u in range(2):
                    i = it * 2 + u
                    pool.wait_ge(r_made, i * 4 + 6)
                    pool.wait_ge(fetched[u], i * TOPK * 8 + (TOPK * 16 - u * TOPK * 8))
                    stage(i + 2, u)
                    pool.wait_ge(acc_made, i + 1)
                    g.tensor_tensor(turn[:, :], half[:, 0:1], half[:, 0:1], ALU.mult)
                    fetch(u)

        @block.scalar
        def _(act):
            for s_ in (h_relu, h_made, y_moved):
                act.sem_inc(s_, 1)
            act.wait_ge(head_in, 32)
            nc.scalar.activation(small[:, 0:1], lam_sb[:, :], ACT.Exp, scale=-1.0).then_inc(lam_act, 1)
            nc.scalar.activation(small[:, 1:2], eta_sb[:, :], ACT.Tanh).then_inc(lam_act, 1)
            def deviations(n):
                act.wait_ge(var_made, n + 1)
                cols = slice(n * NT // 2, (n + 1) * NT // 2)
                nc.scalar.activation(st[:, 2, cols], st[:, 1, cols], ACT.Sqrt).then_inc(sd_made, 1)

            def normalise(n):
                act.wait_ge(scale_made, n + 1)
                for i in range((4 * n + 2) * NT // 8, (n + 1) * NT // 2):
                    ins = nc.scalar.activation(xn[:, i, :], xs[:, i, :], ACT.Identity, scale=st[:, 3, i:i + 1],
                                               bias=st[:, 0, i:i + 1])
                ins.then_inc(xna_made, 1)

            deviations(0)
            normalise(0)
            for g in range(NT // 4):
                if g == 1:
                    deviations(1)
                if g == NT // 8:
                    normalise(1)
                act.wait_ge(xnT_ps, g + 1)
                nc.scalar.copy(flat(xnT[:, 4 * g:4 * g + 4, :]), pst[g % 2]).then_inc(xnT_made, 1)
            act.wait_ge(var_made, 3)
            nc.scalar.activation(ks[:, 1, :], ks[:, 0, :], ACT.Sqrt).then_inc(sd_made, 1)
            act.wait_ge(max_made, 1)
            nc.scalar.activation(pb, pr, ACT.Exp).then_inc(exp_made, 1)

            act.wait_ge(pos_made, 1)
            act.wait_ge(owner_made, 1)
            for g in range(NT // 4):
                act.wait_ge(stat_ps, g + 1)
                nc.scalar.copy(GY[:, :, 0, 32 * g:32 * g + 32].rearrange("p t c -> p c t"),
                               psH[g % 2].rearrange("p (c t) -> p c t", t=TB)).then_inc(stat_made, 1)
            for g in range(NT // 4):
                act.wait_ge(kT_ps, g + 1)
                if g == 0:
                    act.wait_ge(cleared, CLEARS * 16)
                    act.wait_ge(const_in[0], 16)
                nc.scalar.activation(KT[:, :, 32 * g:32 * g + 32].rearrange("p t c -> p c t"),
                                     pst[2 + g % 2].rearrange("p (c t) -> p c t", t=TB), ACT.Copy,
                                     scale=knw_sb[:, 0:1]).then_inc(kT_made, 1)
            act.wait_ge(kT_made, NT // 4)
            nc.scalar.activation(ksq[:, :].rearrange("p (c t) -> p c t", t=TB), KT[:, :, :].rearrange("p t c -> p c t"),
                                 ACT.Square).then_inc(sq_made, 1)
            def to_T(t, k):
                nc.scalar.copy(xT[k], psX).then_inc(xT_made, 1)

            def hidden(t, k):
                nc.scalar.activation(hr[k], psH[k], ACT.Relu).then_inc(h_relu, 1)
                act.wait_ge(h_relu, t + 2)
                nc.scalar.activation(hs[k], hr[k], ACT.Square).then_inc(h_made, 1)

            def slot(t0, j):
                if t0 is None:
                    for k in range(2):
                        act.wait_ge(xT_ps, k + 1)
                        to_T(k, k)
                    act.wait_ge(h_ps, 1)
                    hidden(0, 0)
                    return
                t = t0 + j
                act.wait_ge(xT_ps, t + 3)
                act.wait_ge(h_ps, t + 1)
                to_T(t + 2, j % 2)
                act.wait_ge(h_ps, t + 2)
                act.wait_ge(h_made, t + 1)
                act.wait_ge(y_ps, t + 1)
                hidden(t + 1, (j + 1) % 2)
                act.wait_ge(y_ps, t + 2)
                act.wait_ge(y_out[j % 2], t0 * 8 + (j // 2 * 16 + 16))
                nc.scalar.copy(ys[j % 2], psY).then_inc(y_moved, 1)

            solve_and_slots(act, lambda q, s: None, slot)

            act.wait_ge(gy_made, QT * (TB - 1) - 1)
            act.wait_ge(ys_zero, 2)

            def stage(i, u):
                nc.scalar.copy(GS[u].rearrange("p (b r t) -> p b r t", b=B, r=2),
                               tile_blocks(GY[:, :, 0, :], i)).then_inc(staged_y, 1)
                for r in range(2):
                    nc.scalar.copy(YS[u][:, r, :].rearrange("p (b r t) -> p b r t", b=B, r=2)[:, :, r, :],
                                   tile_blocks(GY[:, :, 1, :], i)[:, :, r, :]).then_inc(staged_y, 1)

            for u in range(2):
                stage(u, u)

            act.wait_ge(ux_zero, 2)

            def deviation(i):
                act.wait_ge(yvar_made, i + 1)
                nc.scalar.activation(ysd[:, :], ymv[:, 1:2], ACT.Sqrt, bias=small[:, 5:6]).then_inc(ysd_made, 1)

            def shared_relu(i):
                act.wait_ge(sh_ps, i + 1)
                act.wait_ge(sh_made, i)
                nc.scalar.activation(hr[0], psSH, ACT.Relu).then_inc(sh_relu, 1)

            def shared_square(i):
                act.wait_ge(sh_relu, i + 1)
                if not isinstance(i, int) or i:
                    act.wait_ge(sy_ps, i)
                nc.scalar.activation(hs[0], hr[0], ACT.Square).then_inc(sh_made, 1)

            def g_out(i, u, r):
                if not isinstance(i, int) or i or r:
                    act.wait_ge(r_ps, i * 2 + r)
                act.wait_ge(u_ps, i * 4 + (r * 2 + 1))
                for b in range(2):
                    rows = slice(b * TS, (b + 1) * TS)
                    ins = nc.scalar.copy(UX[u][rows, b, :], psU[u][rows, :])
                ins.then_inc(ua_made, 1)

            def pass_tile(i, u, more, first):
                g_out(i, u, 0)
                shared_square(i)
                g_out(i, u, 1)
                if not first:
                    deviation(i - 1)
                if more:
                    shared_relu(i + 1)
                if more > 1:
                    act.wait_ge(u_ps, i * 4 + 4)
                    stage(i + 2, u)

            act.wait_ge(sh_ps, 1)
            nc.scalar.activation(hr[0], psSH, ACT.Relu).then_inc(sh_relu, 1)
            for u in range(2):
                pass_tile(u, u, 2, u == 0)
            with act.Fori(1, NT // 2 - 1) as it:
                for u in range(2):
                    pass_tile(it * 2 + u, u, 2, False)
            for u in range(2):
                pass_tile(NT - 2 + u, u, 1 - u, False)
            deviation(NT - 1)

        @block.vector
        def _(dve):
            c = Count(dve_c)

            def link(ins):
                dve.wait_ge(dve_c, c.up(ins))

            v = nc.vector
            s_ = Count(stats_made)
            for n in range(2):
                dve.wait_ge(x_in[n], 64)
                cols = slice(n * NT // 2, (n + 1) * NT // 2)
                for i in range(n * NT // 2, (n + 1) * NT // 2):
                    s_.up(v.bn_stats(bst[:, i, :], xs[:, i, :]))
                dve.wait_ge(stats_made, s_.n)
                for i in range(n * NT // 2, (n + 1) * NT // 2):
                    s_.up(v.bn_aggr(mv[:, i, :], bst[:, i, :]))
                dve.wait_ge(stats_made, s_.n)
                v.tensor_scalar(st[:, 1, cols], mv[:, cols, 1], LN_EPS, None, ALU.add).then_inc(var_made, 1)
                dve.wait_ge(sd_made, n + 1)
                link(v.reciprocal(st[:, 3, cols], st[:, 2, cols]))
                v.scalar_tensor_tensor(st[:, 0, cols], mv[:, cols, 0], -1.0, st[:, 3, cols],
                                       ALU.mult, ALU.mult).then_inc(scale_made, 1)
                for i in range(n * NT // 2, (4 * n + 2) * NT // 8):
                    ins = v.tensor_scalar(xn[:, i, :], xs[:, i, :], mv[:, i, 0:1], st[:, 3, i:i + 1],
                                          ALU.subtract, ALU.mult)
                    if i < (4 * n + 2) * NT // 8 - 1:
                        c.up(ins)
                ins.then_inc(xn_made, 1)
            dve.wait_ge(xn_made, 2)
            dve.wait_ge(xna_made, 2)
            v.tensor_tensor(tmp[:, :], flat(xn[:, :, :]), flat(xn[:, :, :]), ALU.mult).then_inc(sq_made, 1)
            dve.wait_ge(sq_made, 1)
            v.tensor_reduce(ks[:, 1, :], tmp[:, :].rearrange("p (i k) -> p i k", k=HD), AX.X, ALU.add).then_inc(sq_made, 1)
            dve.wait_ge(sq_made, 2)
            v.tensor_scalar(ks[:, 0, :], ks[:, 1, :], 1.0 / HD, RMS_EPS, ALU.mult, ALU.add).then_inc(var_made, 1)

            def over_e(ap):
                return ap.unsqueeze(2).to_broadcast([P, NT, E])

            def by_e(ap):
                return ap.rearrange("p (i e) -> p i e", e=E)

            dve.wait_ge(logits_ps, 1)
            lg = by_e(pslog)
            link(v.tensor_reduce(st[:, 0, :], lg, AX.X, ALU.max))
            v.tensor_tensor(pr, lg, over_e(st[:, 0, :]), ALU.subtract).then_inc(max_made, 1)
            dve.wait_ge(exp_made, 1)
            link(v.tensor_reduce(st[:, 0, :], pb, AX.X, ALU.add))
            link(v.reciprocal(st[:, 1, :], st[:, 0, :]))
            link(v.tensor_tensor(pr, pb, over_e(st[:, 1, :]), ALU.mult))
            dve.wait_ge(iotas_made, 3)
            rankb = rank[:, :].unsqueeze(1).to_broadcast([P, NT, E])
            for k in range(TOPK):
                link(v.tensor_reduce(wgt[:, k, :], pr, AX.X, ALU.max))
                link(v.tensor_tensor(pb, pr, over_e(wgt[:, k, :]), ALU.is_equal))
                link(v.tensor_tensor(pb, pb, rankb, ALU.mult))
                link(v.tensor_reduce(st[:, 2, :], pb, AX.X, ALU.max))
                link(v.tensor_tensor(pick[k], pb, over_e(st[:, 2, :]), ALU.is_equal))
                if k == 0:
                    link(v.scalar_tensor_tensor(pr, pick[0], -2.0, pr, ALU.mult, ALU.add))
            v.tensor_tensor(both, pick[0], pick[1], ALU.add).then_inc(both_made, 1)
            link(v.tensor_tensor(st[:, 2, :], wgt[:, 0, :], wgt[:, 1, :], ALU.add))
            link(v.tensor_scalar(st[:, 2, :], st[:, 2, :], 1e-9, None, ALU.max))
            link(v.reciprocal(st[:, 3, :], st[:, 2, :]))
            link(v.tensor_tensor(wgt[:, :, :], wgt[:, :, :], st[:, 3:4, :].to_broadcast([P, TOPK, NT]), ALU.mult))
            dve.wait_ge(counts_ps, 1)
            link(v.tensor_copy(total, by_e(pstotal)))
            for e in range(E):
                c.up(v.tensor_tensor_scan(upto[:, e, :], ones[:, 0:NT], total[:, :, e], 0.0, ALU.mult, ALU.add))
            dve.wait_ge(dve_c, c.n)
            link(v.tensor_tensor(need, upto[:, :, NT - 1:NT].to_broadcast([P, E, NT]),
                                 steps[:, :].unsqueeze(1).to_broadcast([P, E, NT]), ALU.is_gt))
            link(v.tensor_reduce(tiles[:, 0, :], need, AX.X, ALU.add))
            link(v.tensor_tensor_scan(tiles[:, 1, :], ones[:, 0:E], tiles[:, 0, :], 0.0, ALU.mult, ALU.add))
            link(v.tensor_tensor(tiles[:, 2, :], tiles[:, 1, :], tiles[:, 0, :], ALU.subtract))
            uptov = upto.rearrange("p e i -> p i e")
            link(v.tensor_tensor(pb, uptov, total, ALU.subtract))
            link(v.tensor_tensor(pb, pb, by_e(psbefore), ALU.add))
            link(v.scalar_tensor_tensor(pb, tiles[:, 2:3, :].to_broadcast([P, NT, E]), float(P), pb,
                                        ALU.mult, ALU.add))
            for k in range(TOPK):
                link(v.tensor_tensor(pr, pick[k], pb, ALU.mult))
                link(v.tensor_reduce(pos_f[:, :, k:k + 1], pr, AX.X, ALU.add))
            v.tensor_copy(pos[:, :, :], pos_f).then_inc(pos_made, 1)
            nsl = SLOTS + AHEAD
            link(v.tensor_tensor(past, slot_no.unsqueeze(2).to_broadcast([P, nsl, E]),
                                 tiles[:, 1:2, :].to_broadcast([P, nsl, E]), ALU.is_ge))
            link(v.tensor_reduce(owner_f, past, AX.X, ALU.add))
            link(v.tensor_scalar(owner_f, owner_f, float(E - 1), None, ALU.min))
            v.tensor_copy(owner[:, :], owner_f).then_inc(owner_made, 1)

            dve.wait_ge(sd_made, 3)
            link(v.reciprocal(ks[:, 0, :], ks[:, 1, :]))
            knv = kn[:, :, :].rearrange("p i (h k) -> p (i h) k", k=HD)
            v.tensor_tensor(knv, xn[:, :, :].rearrange("p i (h k) -> p (i h) k", k=HD),
                            ks[:, 0, :].unsqueeze(2).to_broadcast([P, NT * H, HD]), ALU.mult).then_inc(kn_made, 1)

            gathered = tmp[:, NT // 2 * D:NT // 2 * D + (TB - 1) * 2 * QB].rearrange("p (t g c) -> p t g c", g=2, c=QB)
            prod = tmp[:, 0:(TB - 1) * 2 * QB].rearrange("p (t g c) -> p t g c", g=2, c=QB)

            def products(s):
                n = TB - 1 - s
                cols = slice(0, QB)
                if s > 1:
                    dve.wait_ge(gram_ps, s)
                v.tensor_tensor(kp_of(s), KT[:, s + 1:TB, cols],
                                KT[:, s:s + 1, cols].to_broadcast([P, n, QB]), ALU.mult).then_inc(kp_made, 1)

            q_ = Count(const_made)

            def qlink(ins):
                dve.wait_ge(const_made, q_.up(ins))

            dve.wait_ge(masks_made, MASKS)
            dve.wait_ge(lam_act, 2)
            qlink(v.tensor_scalar(small[:, 2:3], small[:, 0:1], 1.0, None, ALU.add))
            q_.up(v.memset(powr[:, 0:1], 1.0))
            q_.up(v.memset(small[:, 5:6], LN_EPS))
            qlink(v.reciprocal(powr[:, 1:2], small[:, 2:3]))
            qlink(v.tensor_scalar(small[:, 3:4], powr[:, 1:2], -1.0, 1.0, ALU.mult, ALU.add))
            qlink(v.tensor_scalar(small[:, 4:5], small[:, 3:4], small[:, 1:2], 1.0 / HD, ALU.mult, ALU.mult))
            n = 1
            while n < TB:
                qlink(v.tensor_scalar(powr[:, n + 1:2 * n + 1], powr[:, 1:n + 1], powr[:, n:n + 1], None, ALU.mult))
                n *= 2
            qlink(v.tensor_scalar(cpow[:, :], powr[:, :], small[:, 4:5], None, ALU.mult))
            q_.up(v.tensor_scalar(decay[:, :], ident[:, :], powr[:, TB:TB + 1], None, ALU.mult))
            dve.wait_ge(const_in[0], 16)
            qlink(v.tensor_scalar(cpw[:, :], cpow[:, 0:TB], knw_sb[:, 0:1], None, ALU.mult))
            for t in range(TB):
                q_.up(v.tensor_copy(keywT[:, :].rearrange("p (a t) -> p a t", t=TB)[:, :, t:t + 1],
                                    cpw[:, TB - 1 - t:TB - t].unsqueeze(1).to_broadcast([P, P // TB, 1])))
            q_.up(v.tensor_scalar(csel[:, :], same[:, :].rearrange("p (h k) -> p k h", k=HD)[:, 0, :], small[:, 4:5], None, ALU.mult))
            assert q_.n == CONSTS, q_.n
            v.tensor_scalar(headsum[:, :], same[:, :], cpow[:, 1:2], None, ALU.mult).then_inc(headsum_made, 1)

            dve.wait_ge(keywT_made, 1)
            link(v.tensor_reduce(half[:, 0:1], ident[:, :].rearrange("p (b r t) -> p b r t", b=B, r=2)[:, :, 0, :],
                                 AX.XY, ALU.add))
            link(v.tensor_scalar(half[:, 1:2], half[:, 0:1], -1.0, 1.0, ALU.mult, ALU.add))
            for r in range(2):
                v.tensor_scalar(keyw[:, r, :], pskw, half[:, r:r + 1], None, ALU.mult).then_inc(keyw_moved, 1)
            dve.wait_ge(kT_made, NT // 4)
            products(0)
            products(1)
            dve.wait_ge(stat_made, NT // 4)
            dve.sem_inc(gy_made, 1)

            def solve(q, s):
                n = TB - 1 - s
                step = q * (TB - 1) + s
                cols = bass.ds(q * QB, QB)
                if s == 0:
                    v.tensor_tensor(GY[:, :, 1, cols], KT[:, :, cols], powr[:, 1:TB + 1].unsqueeze(2).to_broadcast([P, TB, QB]),
                                    ALU.mult).then_inc(y0_made, 1)
                    dve.wait_ge(y0_made, q + 1)
                dve.wait_ge(gram_ps, step + 2)
                dve.wait_ge(gy_made, step + 1)
                gram = gram_of(s).rearrange("p (t o c) -> p t o c", o=1, c=QB)
                v.tensor_tensor(prod[:, 0:n] if s else gathered, gram.to_broadcast([P, n, 2, QB]),
                                GY[:, s:s + 1, :, cols].to_broadcast([P, n, 2, QB]), ALU.mult).then_inc(gram_used, 1)
                if isinstance(q, int) and step + 2 < TB - 1:
                    products(step + 2)
                dve.wait_ge(gram_used, step + 1)
                if s:
                    v.scalar_tensor_tensor(gathered[:, s:], gathered[:, s:], powr[:, 1:2], prod[:, 0:n],
                                           ALU.mult, ALU.add).then_inc(gather_made, 1)
                    dve.wait_ge(gather_made, q * (TB - 2) + s)
                v.tensor_tensor(GY[:, s + 1:s + 2, :, cols], GY[:, s + 1:s + 2, :, cols], gathered[:, s:s + 1],
                                ALU.add).then_inc(gy_made, 1)
                if isinstance(q, int) and step == NT // FACT:
                    dve.wait_ge(fac_ps, NT // FACT)
                    v.tensor_scalar(flat(fac[:, :, :]), psfac, 1.0, None, ALU.add).then_inc(fac_read, 1)

            solve_and_slots(dve, solve, lambda t0, j: None)
            dve.wait_ge(gy_made, QT * (TB - 1) + 1)

            dve.wait_ge(xs_made, 1)

            def llink(ins, i, n):
                ins.then_inc(pass_c, 1)
                dve.wait_ge(pass_c, i * LINKS + n)

            def tile_of(t3, i):
                return t3[:, bass.ds(i, 1), :].rearrange("p o d -> p (o d)")

            def g_out(i, u, r):
                dve.wait_ge(u_ps, i * 4 + (r * 2 + 2))
                for b in range(2, B):
                    rows = slice(b * TS, (b + 1) * TS)
                    ins = v.tensor_copy(UX[u][rows, b, :], psU[u][rows, :])
                ins.then_inc(uv_made, 1)

            def mask_state(i, r):
                dve.wait_ge(r_ps, i * 2 + (r + 1))
                for b in range(0, B, 2):
                    v.tensor_tensor(R[:, b:b + 2, :].rearrange("p b (g c) -> p b g c", g=HG),
                                    psR[:, b * GW:(b + 2) * GW].rearrange("p (b o c) -> p b o c", o=1, c=GW).to_broadcast([P, 2, HG, GW]),
                                    same[:, :].rearrange("p (o g c) -> p o g c", o=1, c=GW).to_broadcast([P, 2, HG, GW]),
                                    ALU.mult).then_inc(r_made, 1)

            def norm_a(i, u):
                dve.wait_ge(ua_made, i * 2 + 2)
                v.tensor_tensor(yb[u].rearrange("p (h k) -> p h k", k=HD), psU[u].rearrange("p (h k) -> p h k", k=HD),
                                tile_of(fac, i).unsqueeze(2).to_broadcast([P, H, HD]), ALU.mult).then_inc(t_read, 1)

            def norm_b(i, u):
                dve.wait_ge(t_read, i + 2)
                v.bn_stats(yst[:, :], yb[u]).then_inc(pass_c, 1)

            def norm_c(i, u):
                dve.wait_ge(pass_c, i * LINKS + 1)
                dve.wait_ge(sy_ps, i + 1)
                dve.wait_ge(fetched[u], i * TOPK * 8 + (TOPK * 16 - u * TOPK * 8))
                v.scalar_tensor_tensor(acc, gy[u][0][:, :], wgt[:, 0, bass.ds(i, 1)], psS[u],
                                       ALU.mult, ALU.add).then_inc(pass_c, 1)
                v.bn_aggr(ymv[:, 0:2], yst[:, :]).then_inc(yvar_made, 1)

                dve.wait_ge(pass_c, i * LINKS + 2)
                v.scalar_tensor_tensor(acc, gy[u][1][:, :], wgt[:, 1, bass.ds(i, 1)], acc,
                                       ALU.mult, ALU.add).then_inc(acc_made, 1)

            def norm_d(i, u):
                dve.wait_ge(yvar_made, i + 1)
                v.scalar_tensor_tensor(yb[u], yb[u], ymv[:, 0:1], onw_sb[:, :], ALU.subtract, ALU.mult).then_inc(pass_c, 1)

            def norm_e(i):
                dve.wait_ge(ysd_made, i + 1)
                v.reciprocal(ymv[:, 3:4], ysd[:, :]).then_inc(pass_c, 1)

            def norm_f(i, u):
                dve.wait_ge(pass_c, i * LINKS + 4)
                dve.wait_ge(acc_made, i + 1)
                dve.wait_ge(out_done[u], i * (B * 8) + (16 - u * B * 8))
                v.scalar_tensor_tensor(yo[u], yb[u], ymv[:, 3:4], acc, ALU.mult, ALU.add).then_inc(yo_made, 1)

            def pass_tile(i, u, before):
                g_out(i, u, 0)
                if before > 1:
                    norm_e(i - 2)
                if before:
                    norm_a(i - 1, 1 - u)
                if before > 1:
                    norm_f(i - 2, u)
                mask_state(i, 0)
                if before > 1:
                    dve.wait_ge(yo_made, i - 1)
                if before:
                    norm_b(i - 1, 1 - u)
                g_out(i, u, 1)
                if before:
                    norm_c(i - 1, 1 - u)
                mask_state(i, 1)
                if before:
                    norm_d(i - 1, 1 - u)

            dve.wait_ge(ux_zero, 2)
            dve.sem_inc(t_read, 1)
            for u in range(2):
                pass_tile(u, u, u)
            with dve.Fori(1, NT // 2) as it:
                for u in range(2):
                    pass_tile(it * 2 + u, u, 2)
            norm_e(NT - 2)
            norm_a(NT - 1, 1)
            norm_f(NT - 2, 0)
            dve.wait_ge(yo_made, NT - 1)
            for piece in norm_b, norm_c, norm_d:
                piece(NT - 1, 1)
            norm_e(NT - 1)
            norm_f(NT - 1, 1)

        @block.tensor
        def _(pe):
            mm, tr = nc.tensor.matmul, nc.tensor.transpose
            for s_ in (gram_ps, y_ps):
                pe.sem_inc(s_, 1)
            pe.wait_ge(masks_made, MASKS)

            def logits(g):
                pe.wait_ge(xnT_made, g + 1)
                for i in range(4 * g, 4 * g + 4):
                    ins = mm(pslog[:, E * i:E * i + E], xnT[:, i, :], rw_sb[:, :], start=True, stop=True)
                if g == NT // 4 - 1:
                    ins.then_inc(logits_ps, 1)

            for g in range(NT // 4):
                if g % (NT // 8) == 0:
                    pe.wait_ge(xn_made, g // (NT // 8) + 1)
                    pe.wait_ge(xna_made, g // (NT // 8) + 1)
                if g >= 2:
                    pe.wait_ge(xnT_made, g - 1)
                for j in range(4):
                    ins = tr(pst[g % 2][:, P * j:P * j + P], xn[:, 4 * g + j, :], ident[:, :])
                ins.then_inc(xnT_ps, 1)
                if g == 0:
                    pe.wait_ge(w_in, 32)
                else:
                    logits(g - 1)
            logits(NT // 4 - 1)

            def static(g):
                if g >= 2:
                    pe.wait_ge(stat_made, g - 1)
                mm(psH[g % 2], w_sb[:, :], flat(xnT[:, 4 * g:4 * g + 4, :]), start=True, stop=True).then_inc(stat_ps, 1)

            pe.wait_ge(both_made, 1)
            mm(psbefore, before[:, :], flat(both), start=True, stop=True)
            mm(pstotal, ones[:, :], flat(both), start=True, stop=True).then_inc(counts_ps, 1)
            for g in range(NT // 4):
                static(g)
            pe.wait_ge(kn_made, 1)
            for g in range(NT // 4):
                if g == NT // 4 - 2:
                    pe.wait_ge(const_made, CONSTS)
                    tr(pskw, keywT[:, :], ident[:, :]).then_inc(keywT_made, 1)
                if g >= 2:
                    pe.wait_ge(kT_made, g - 1)
                for j in range(4):
                    ins = tr(pst[2 + g % 2][:, P * j:P * j + P], kn[:, 4 * g + j, :], ident[:, :])
                ins.then_inc(kT_ps, 1)
            pe.wait_ge(headsum_made, 1)

            def solve(q, s):
                n = TB - 1 - s
                step = q * (TB - 1) + s
                pe.wait_ge(kp_made, step + 1)
                if not isinstance(q, int) or step >= 2:
                    pe.wait_ge(gram_used, step - 2 if s == 0 else step - 1)
                for t in range(0, n, 512 // QB):
                    m = min(512 // QB, n - t)
                    ins = mm(gram_of(s)[:, t * QB:(t + m) * QB], headsum[:, :], flat(kp_of(s)[:, t:t + m, :]),
                             start=True, stop=True)
                ins.then_inc(gram_ps, 1)
                if isinstance(q, int) and step < NT // FACT:
                    pe.wait_ge(sq_made, 3)
                    pe.wait_ge(pos_made, 1)
                    for i in range(step * FACT, (step + 1) * FACT):
                        ins = mm(psfac[:, H * i:H * i + H], ksq[:, i * P:(i + 1) * P], csel[:, :], start=True, stop=True)
                    ins.then_inc(fac_ps, 1)

            def to_T(t, k):
                tr(psX, xg[k], ident[:, :]).then_inc(xT_ps, 1)

            def up(t, k):
                for f in range(FC):
                    ins = mm(psH[k % 2][:, f * P:f * P + P], wst[k][:, f * P:f * P + P], xT[k % 2], start=True, stop=True)
                ins.then_inc(h_ps, 1)

            def slot(t0, j):
                if t0 is None:
                    pe.wait_ge(owner_made, 1)
                    pe.wait_ge(routed_in, 16)
                    pe.wait_ge(stat_made, NT // 4)
                    pe.wait_ge(fac_read, 1)
                    pe.wait_ge(keyw_moved, 2)
                    for k in range(2):
                        pe.wait_ge(xg_in[k], 16)
                        if k:
                            pe.wait_ge(xT_made, k)
                        to_T(k, k)
                    pe.wait_ge(xT_made, 1)
                    pe.wait_ge(w_fetched[0], 16)
                    up(0, 0)
                    return
                t = t0 + j
                pe.wait_ge(xg_in[(j + 2) % AHEAD], t0 * 4 + ((j + 2) // AHEAD * 16 + 16))
                pe.wait_ge(xT_made, t + 2)
                to_T(t + 2, (j + 2) % AHEAD)
                pe.wait_ge(w_fetched[(j + 1) % AHEAD], t0 * 4 + ((j + 1) // AHEAD * 16 + 16))
                pe.wait_ge(h_relu, t + 1)
                up(t + 1, (j + 1) % AHEAD)
                e = pe.value_load(owner[0:1, bass.ds(t, 1)], min_val=0, max_val=E - 1)
                pe.wait_ge(h_made, t + 2)
                pe.wait_ge(y_moved, t + 1)
                for f in range(FC):
                    ins = mm(psY, hs[j % 2][:, f * P:f * P + P],
                             pj_sb[:, bass.ds(e, 1), f, :].rearrange("p o d -> p (o d)"), start=(f == 0), stop=(f == FC - 1))
                ins.then_inc(y_ps, 1)

            solve_and_slots(pe, solve, slot)

            pe.wait_ge(gram_used, QT * (TB - 1) - 1)
            pe.wait_ge(h_relu, SLOTS + 2)
            pe.wait_ge(y_moved, SLOTS + 1)

            def g_start(i, u):
                pe.wait_ge(staged_y, i * 3 + 3)
                mm(psU[u], GS[u], ident[:, :], start=True, stop=False, skip_group_check=True)

            g_start(0, 0)

            def shared_up(i, chunks):
                for f in chunks:
                    ins = mm(psSH[:, f * P:f * P + P], sfc_sb[:, f * P:f * P + P],
                             xnT[:, bass.ds(i, 1), :].rearrange("p o t -> p (o t)"), start=True, stop=True)
                if f == FC - 1:
                    ins.then_inc(sh_ps, 1)

            def shared_start(i, u):
                mm(psS[u], ident[:, :], xs[:, bass.ds(i, 1), :].rearrange("p o d -> p (o d)"), start=True, stop=False)

            def shared_down(u, chunks):
                for f in chunks:
                    ins = mm(psS[u], hs[0][:, f * P:f * P + P], spj_sb[:, f, :], start=False, stop=(f == FC - 1))
                if f == FC - 1:
                    ins.then_inc(sy_ps, 1)

            pe.wait_ge(shared_in, 32)
            pe.wait_ge(xs_made, 1)
            shared_up(0, range(FC))

            def pass_tile(i, u, more):
                for r in range(2):
                    for b in range(B):
                        if b % 2 == 0:
                            pe.wait_ge(r_made, i * 4 + (r * 2 + b // 2 + 1))
                        rows = slice(b * TS, (b + 1) * TS)
                        ins = mm(psU[u][rows, :], YS[u][:, r, rows], R[:, b, :], start=False, stop=True, skip_group_check=True)
                        if b % 2:
                            ins.then_inc(u_ps, 1)
                    for g in range(HG):
                        heads = slice(g * GW, (g + 1) * GW)
                        mm(psR[heads, :], decay[:, heads], R[:, :, heads], start=True, stop=False, skip_group_check=True)
                    if r == 0:
                        if more:
                            pe.wait_ge(sh_relu, i + 1)
                            shared_up(i + 1, [0, 1])
                        pe.wait_ge(staged, i + 1)
                    else:
                        pe.wait_ge(sh_made, i + 1)
                        shared_down(u, [0, 1])
                    pe.wait_ge(ua_made, i * 2 + (r + 1))
                    pe.wait_ge(uv_made, i * 2 + (r + 1))
                    for g in range(HG):
                        heads = slice(g * GW, (g + 1) * GW)
                        ins = mm(psR[heads, :], KS[u][:, r, heads], UX[u][:, :, heads], start=False, stop=True, skip_group_check=True)
                    ins.then_inc(r_ps, 1)
                    if r == 1:
                        if more:
                            g_start(i + 1, 1 - u)
                        shared_down(u, [2, 3])
                    else:
                        if more:
                            shared_up(i + 1, [2, 3])
                        pe.wait_ge(t_read, i + 1)
                        shared_start(i, u)

            with pe.Fori(0, NT // 2 - 1) as it:
                for u in range(2):
                    pass_tile(it * 2 + u, u, True)
            for u in range(2):
                pass_tile(NT - 2 + u, u, u == 0)


MASKS = 8
CONSTS = 1 + 1 + 1 + 3 + 4 + 1 + 1 + 1 + TB + 1
CLEARS = -(-(SLOTS + AHEAD) // NT)
LINKS = 4


def kernel(L0_attn_x, L0_attn_W, L0_attn_k_norm_w, L0_attn_o_norm_w, L0_attn_o_norm_b, L0_attn_eta_raw,
           L0_attn_lam_logit, L0_ffn_router_w, L0_ffn_w_fc, L0_ffn_w_proj, L0_ffn_shared_fc, L0_ffn_shared_proj):
    import concourse.bacc as bacc
    from concourse.bass_utils import run_bass_kernel_spmd

    def lay(a, order=None, shape=None):
        a = np.asarray(a)
        if shape:
            a = a.reshape(shape)
        return np.ascontiguousarray(a.transpose(order) if order else a)

    ins = {
        "x": lay(L0_attn_x),
        "wT": lay(L0_attn_W, (1, 0)),
        "knw": lay(L0_attn_k_norm_w), "onw": lay(L0_attn_o_norm_w), "onb": lay(L0_attn_o_norm_b),
        "eta": lay(L0_attn_eta_raw), "lam": lay(L0_attn_lam_logit),
        "rwT": lay(L0_ffn_router_w, (1, 0)),
        "fcT": lay(L0_ffn_w_fc, (2, 0, 1)),
        "pjT": lay(L0_ffn_w_proj, (3, 0, 2, 1), (E, D, FC, P)),
        "sfcT": lay(L0_ffn_shared_fc, (1, 0)),
        "spjT": lay(L0_ffn_shared_proj, (2, 1, 0), (D, FC, P)),
    }
    nc = bacc.Bacc("TRN2", target_bir_lowering=False, num_devices=1)
    aps = [nc.dram_tensor(n, a.shape, mybir.dt.from_np(a.dtype), kind="ExternalInput").ap() for n, a in ins.items()]
    out = nc.dram_tensor("out", (B, L, D), F32, kind="ExternalOutput").ap()
    build(nc, *aps, out)
    r = run_bass_kernel_spmd(nc, [ins], core_ids=[0])
    return r.results[0]["out"]
```
